# Optimizing a Trainium2 kernel written in Bass

```python
import numpy as np
import jax
import jax.numpy as jnp

def _softmax(x, axis=-1):
    return jax.nn.softmax(x, axis=axis)

def _gelu(x):
    return jax.nn.gelu(x, approximate=True)

def _silu(x):
    return jax.nn.silu(x)

def _sigmoid(x):
    return jax.nn.sigmoid(x)

def _layernorm(x, axis=-1, eps=1e-05):
    m = jnp.mean(x, axis=axis, keepdims=True)
    v = jnp.var(x, axis=axis, keepdims=True)
    return (x - m) / jnp.sqrt(v + eps)

def _scatter_add(tgt, idx, src, axis=0):
    return tgt.at[idx].add(src)

def _segment_sum(src, seg, n):
    return jax.ops.segment_sum(src, seg, n)
kernel_name = 'mk_gnn_preln_d1_gnn_r8_98befa'

def setup_inputs(seed: int=0):
    np.random.seed(seed)
    _w = jnp.asarray

    def _rec_inputs():
        import jax
        import jax.numpy as jnp
        _gk = jax.random.key(seed)
        x = -0.000202 + 1 * jax.random.normal(jax.random.fold_in(_gk, 1), (6250, 128), jnp.float32)
        _s = jax.random.randint(jax.random.fold_in(_gk, 2), (100000,), 0, 6250, jnp.int32)
        _d = jax.random.randint(jax.random.fold_in(_gk, 3), (100000,), 0, 6250, jnp.int32)
        _loop = jnp.arange(6250, dtype=jnp.int32)
        src = jnp.concatenate([_s, _d, _loop])
        dst = jnp.concatenate([_d, _s, _loop])
        _o = jnp.argsort(dst, stable=True)
        src = src[_o]
        dst = dst[_o]
        edge_attr_32 = -5.3897e-05 + 0.999841 * jax.random.normal(jax.random.fold_in(_gk, 12), (206250, 32), jnp.float32)
        return (x, src, dst, edge_attr_32)
    x, src, dst, edge_attr_32 = _rec_inputs()

    def _L0_gnn_setup():
        import jax, jax.numpy as jnp
        import numpy as np
        EPS = 1e-06

        def _mlp(x, W1, b1, g, bln, W2, b2):
            h = x @ W1 + b1
            mu = jnp.mean(h, axis=-1, keepdims=True)
            var = jnp.var(h, axis=-1, keepdims=True)
            h = (h - mu) * jax.lax.rsqrt(var + EPS) * g + bln
            h = jax.nn.relu(h)
            return h @ W2 + b2
        key = jax.random.key(seed)
        ks = jax.random.split(key, 12)
        N, E, D, De, H = (6250, 100000, 128, 32, 128)
        s = lambda fan_in: 1.0 / np.sqrt(fan_in)
        return {'nodes': jax.random.normal(ks[0], (N, D), jnp.float32), 'edges': jax.random.normal(ks[1], (E, De), jnp.float32), 'senders': jax.random.randint(ks[2], (E,), 0, N, jnp.int32), 'receivers': jax.random.randint(ks[3], (E,), 0, N, jnp.int32), 'We1': jax.random.normal(ks[4], (D + De, H), jnp.float32) * s(D + De), 'be1': jnp.zeros((H,), jnp.float32), 'ge1': jnp.ones((H,), jnp.float32), 'ble1': jnp.zeros((H,), jnp.float32), 'We2': jax.random.normal(ks[5], (H, H), jnp.float32) * s(H), 'be2': jnp.zeros((H,), jnp.float32), 'Wn1': jax.random.normal(ks[6], (D + H, H), jnp.float32) * s(D + H), 'bn1': jnp.zeros((H,), jnp.float32), 'gn1': jnp.ones((H,), jnp.float32), 'bln1': jnp.zeros((H,), jnp.float32), 'Wn2': jax.random.normal(ks[7], (H, D), jnp.float32) * s(H), 'bn2': jnp.zeros((D,), jnp.float32)}
    _L0_gnn_all = _L0_gnn_setup()
    _L0_gnn_in = {k: v for k, v in _L0_gnn_all.items() if k in ('We1', 'be1', 'ge1', 'ble1', 'We2', 'be2', 'Wn1', 'bn1', 'gn1', 'bln1', 'Wn2', 'bn2')}
    del _L0_gnn_all
    return {'x': x, 'src': src, 'dst': dst, 'edge_attr_32': edge_attr_32, 'L0_gnn_We1': _L0_gnn_in['We1'], 'L0_gnn_be1': _L0_gnn_in['be1'], 'L0_gnn_ge1': _L0_gnn_in['ge1'], 'L0_gnn_ble1': _L0_gnn_in['ble1'], 'L0_gnn_We2': _L0_gnn_in['We2'], 'L0_gnn_be2': _L0_gnn_in['be2'], 'L0_gnn_Wn1': _L0_gnn_in['Wn1'], 'L0_gnn_bn1': _L0_gnn_in['bn1'], 'L0_gnn_gn1': _L0_gnn_in['gn1'], 'L0_gnn_bln1': _L0_gnn_in['bln1'], 'L0_gnn_Wn2': _L0_gnn_in['Wn2'], 'L0_gnn_bn2': _L0_gnn_in['bn2']}

def reference(x, src, dst, edge_attr_32, L0_gnn_We1, L0_gnn_be1, L0_gnn_ge1, L0_gnn_ble1, L0_gnn_We2, L0_gnn_be2, L0_gnn_Wn1, L0_gnn_bn1, L0_gnn_gn1, L0_gnn_bln1, L0_gnn_Wn2, L0_gnn_bn2):
    import jax
    import jax.numpy as jnp

    def _L0_gnn_ref(nodes, edges, senders, receivers, We1, be1, ge1, ble1, We2, be2, Wn1, bn1, gn1, bln1, Wn2, bn2):
        import jax, jax.numpy as jnp
        import numpy as np
        EPS = 1e-06

        def _mlp(x, W1, b1, g, bln, W2, b2):
            h = x @ W1 + b1
            mu = jnp.mean(h, axis=-1, keepdims=True)
            var = jnp.var(h, axis=-1, keepdims=True)
            h = (h - mu) * jax.lax.rsqrt(var + EPS) * g + bln
            h = jax.nn.relu(h)
            return h @ W2 + b2
        N = nodes.shape[0]
        H = We2.shape[1]
        edge_input = jnp.concatenate([nodes[senders], edges], axis=-1)
        messages = _mlp(edge_input, We1, be1, ge1, ble1, We2, be2)
        aggregated = jnp.zeros((N, H), messages.dtype).at[receivers].add(messages)
        counts = jnp.zeros((N,), messages.dtype).at[receivers].add(1.0)
        aggregated = aggregated / jnp.maximum(counts, 1.0)[:, None]
        node_input = jnp.concatenate([nodes, aggregated], axis=-1)
        new_nodes = _mlp(node_input, Wn1, bn1, gn1, bln1, Wn2, bn2)
        return new_nodes + nodes
    h = jnp.maximum(_layernorm(x, axis=-1), 0.0)
    x = x + _L0_gnn_ref(h, edge_attr_32, src, dst, L0_gnn_We1, L0_gnn_be1, L0_gnn_ge1, L0_gnn_ble1, L0_gnn_We2, L0_gnn_be2, L0_gnn_Wn1, L0_gnn_bn1, L0_gnn_gn1, L0_gnn_bln1, L0_gnn_Wn2, L0_gnn_bn2)
    return x

_drawn_inputs = setup_inputs


def setup_inputs(seed=0):
    import zlib

    import numpy as np

    out = dict(_drawn_inputs(seed))
    spreads = {'L0_gnn_be1': (0.0, 0.1),
     'L0_gnn_ge1': (1.0, 0.2),
     'L0_gnn_ble1': (0.0, 0.354),
     'L0_gnn_be2': (0.0, 0.1),
     'L0_gnn_bn1': (0.0, 0.1),
     'L0_gnn_gn1': (1.0, 0.2),
     'L0_gnn_bln1': (0.0, 0.1),
     'L0_gnn_bn2': (0.0, 0.1)}
    factors = {}
    for name, (base, spread) in spreads.items():
        noise = np.random.default_rng([zlib.crc32(name.encode()), seed]).standard_normal(out[name].shape)
        drawn = base * np.exp(spread * noise) if base else spread * noise
        out[name] = jnp.asarray(drawn.astype(out[name].dtype))
    for name, factor in factors.items():
        out[name] = (out[name] * factor).astype(out[name].dtype)
    return out
```

```python
import concourse.bass as bass
from concourse import mybir
from contextlib import ExitStack


def graph_layer(nc, x, src, dst, edge, We1, be1, ge1, ble1, We2, be2, Wn1, bn1, gn1, bln1, Wn2, bn2, out):
    fp32 = mybir.dt.float32
    i32 = mybir.dt.int32
    ALU = mybir.AluOpType
    ACT = mybir.ActivationFunctionType
    AX = mybir.AxisListType

    N, D = x.shape
    E, DE = edge.shape
    H = We2.shape[0]
    P = 128
    EPS_X = 1e-5
    EPS_MLP = 1e-6
    assert D == H == P

    SLOTS = 8
    CHUNK = P * SLOTS
    FULL = E // CHUNK
    TAIL = E - FULL * CHUNK
    TAIL_SLOTS = next(s for s in range(1, SLOTS + 1) if TAIL % s == 0 and TAIL // s <= P)
    TAIL_ROWS = TAIL // TAIL_SLOTS
    PAIRS = FULL // 2
    assert FULL % 2 == 1 and TAIL > 0
    CHUNKS = FULL + 1
    HALF = CHUNKS // 2
    W = 64
    SHIFT = W.bit_length() - 1
    MOST = (N - 1) // W
    PACK = P // DE
    PACKS = SLOTS // PACK

    NR = 125
    TILES = N // NR
    GT = 5
    GROUPS = TILES // GT
    assert TILES * NR == N and GROUPS * GT == TILES and GROUPS % 2 == 0
    GW = GT * D

    table = nc.dram_tensor("sender_table", (N, H), fp32).ap()
    x_v = x.rearrange("(k p) f -> p k f", p=NR)
    out_v = out.rearrange("(k p) f -> p k f", p=NR)
    table_v = table.rearrange("(k p) f -> p k f", p=NR)
    edge_v = edge[0:FULL * CHUNK, :].rearrange("(c p j) f -> c p (j f)", p=P, j=SLOTS)
    src_v = src[0:FULL * CHUNK].rearrange("(c p j) -> c p j", p=P, j=SLOTS)
    dst_v = dst[0:FULL * CHUNK].rearrange("(c p j) -> c p j", p=P, j=SLOTS)
    edge_t = edge[FULL * CHUNK:E, :].rearrange("(p j) f -> p (j f)", j=TAIL_SLOTS)
    src_t = src[FULL * CHUNK:E].rearrange("(p j) -> p j", j=TAIL_SLOTS)
    dst_t = dst[FULL * CHUNK:E].rearrange("(p j) -> p j", j=TAIL_SLOTS)

    ctx = ExitStack()
    with ctx:
        def sb(name, shape, dt=fp32):
            return ctx.enter_context(nc.sbuf_tensor(name, shape, dt))

        def sem(name):
            return ctx.enter_context(nc.semaphore(name))

        def two(name):
            return [sem(f"{name}{b}") for b in range(2)]

        acc = sb("acc", [P, 2, N + W])
        res = sb("res", [NR, TILES, D])
        nodes = sb("nodes", [NR, TILES, 2 * H])
        cen = sb("cen", [P, 6, H])
        CEN_E1, CEN_N1, CEN_BE1, CEN_BN1, CEN_N2, CEN_EDGE = range(6)
        cen_mean = sb("cen_mean", [P, 6])
        vec = sb("vec", [P, 5, H])
        V_GE, V_BE, V_GN, V_BN, V_BO = range(5)
        neg = sb("neg", [P, 2, H])
        cols = sb("cols", [P, 3])
        we2 = sb("we2", [P, H])
        wn2 = sb("wn2", [P, D])
        we2T = sb("we2T", [P, H])
        fused = sb("fused", [P, H])
        shift_col = sb("shift_col", [P, 1])
        shift_row = sb("shift_row", [1, H])
        last_b = sb("last_b", [P, P])
        last_bias = sb("last_bias", [P, D])
        wedge = sb("wedge", [P, PACK, H])
        ident = sb("ident", [P, P])
        ones = sb("ones", [P, P])
        ramp_i = sb("ramp_i", [P, W], i32)
        ramp = sb("ramp", [P, W])

        ends = sb("ends", [HALF, 2, CHUNK], i32)
        lohi = sb("lohi", [HALF, 2, 2])
        spread_diag = sb("spread_diag", [HALF, 2, 2, HALF])
        base = sb("base", [P, CHUNKS])
        base_i = sb("base_i", [1, CHUNKS], i32)
        reach = sb("reach", [1, CHUNKS])
        more_i = sb("more_i", [1, CHUNKS], i32)
        reach_i = sb("reach_i", [1, CHUNKS], i32)

        h_t = [sb(f"h_t{b}", [NR, GW]) for b in range(2)]
        hT = [sb(f"hT{b}", [P, GW]) for b in range(2)]
        bn = [sb(f"bn{b}", [NR, GT, 6]) for b in range(2)]
        mv = [sb(f"mv{b}", [NR, GT, 2]) for b in range(2)]
        small = [sb(f"small{b}", [P, 6, SLOTS]) for b in range(2)]
        S_VAR, S_STD, S_R, S_A, S_B, S_NMR = range(6)

        srcs = [sb(f"srcs{b}", [P, SLOTS], i32) for b in range(2)]
        dsts = [sb(f"dsts{b}", [P, SLOTS], i32) for b in range(2)]
        feat = [sb(f"feat{b}", [P, SLOTS * DE]) for b in range(2)]
        featT = [sb(f"featT{b}", [P, PACKS * P]) for b in range(2)]
        rows = [sb(f"rows{b}", [P, SLOTS, H]) for b in range(2)]
        z = [sb(f"z{b}", [P, SLOTS, H]) for b in range(2)]
        offs = [sb(f"offs{b}", [P, SLOTS]) for b in range(2)]
        onehot = [sb(f"onehot{b}", [P, SLOTS, W]) for b in range(2)]
        squares = [sb(f"squares{b}", [P, SLOTS]) for b in range(2)]
        trash = sb("trash", [P, SLOTS, H])

        agg = [sb(f"agg{b}", [P, GT * NR]) for b in range(2)]
        cnt = [sb(f"cnt{b}", [1, GT * NR]) for b in range(2)]
        u = [z[b][0:NR, 0:GT, :] for b in range(2)]
        uT = hT
        o_t = [h_t[b][:, :].rearrange("p (t c) -> p t c", t=GT) for b in range(2)]

        ps = ctx.enter_context(nc.psum_tensor("ps", [P, 8, 512], fp32))
        flat = ps[:, :, :].rearrange("p b c -> p (b c)")

        def banks(first, width, rows=P):
            return flat[0:rows, 512 * first:512 * first + width]

        ps_hT = banks(0, GW)
        ps_nodes = [banks(2 + 3 * b, 3 * 512) for b in range(2)]
        ps_edge = [banks(2 * b, SLOTS * H) for b in range(2)]
        ps_featT = [banks(4 + b, PACKS * P) for b in range(2)]
        ps_sum = [banks(6 + b, 2 * W) for b in range(2)]
        ps_agg = [banks(2 * b, 1024) for b in range(2)]
        ps_uT = banks(4, GW)
        ps_out = banks(6, GW)

        w_loaded = sem("w_loaded")
        late_loaded = sem("late_loaded")
        cols_loaded = sem("cols_loaded")
        ends_loaded = sem("ends_loaded")
        ident_clear, ident_ready = sem("ident_clear"), sem("ident_ready")
        ones_ready, ramp_made, ramp_ready = sem("ones_ready"), sem("ramp_made"), sem("ramp_ready")
        cen_step, cen_ready = sem("cen_step"), sem("cen_ready")
        prep = sem("prep")
        pe_prep = sem("pe_prep")
        prep_ready = sem("prep_ready")
        x_loaded = two("x_loaded")
        bn_done, bn_seen, aggr_done, nvar_ready, nstd_ready = sem("bn_done"), sem("bn_seen"), sem("aggr_done"), sem("nvar_ready"), sem("nstd_ready")
        nroot = sem("nroot")
        norm_ready = sem("norm_ready")
        h_ready, h_transposed, hT_ready = sem("h_ready"), sem("h_transposed"), sem("hT_ready")
        projected, nodes_ready = sem("projected"), sem("nodes_ready")
        x_plus_h = sem("x_plus_h")
        sums_cleared, res_ready = sem("sums_cleared"), sem("res_ready")
        table_written = two("table_written")
        feat_loaded, src_loaded, dst_loaded = two("feat_loaded"), two("src_loaded"), two("dst_loaded")
        gathered = two("gathered")
        gather_begun = sem("gather_begun")
        feat_transposed, featT_ready, edge_projected = sem("feat_transposed"), sem("featT_ready"), sem("edge_projected")
        offs_ready, onehot_ready, z_ready = sem("offs_ready"), sem("onehot_ready"), sem("z_ready")
        squares_done, var_ready, std_ready = sem("squares_done"), sem("var_ready"), sem("std_ready")
        root = sem("root")
        scaled, message_ready = sem("scaled"), sem("message_ready")
        sums_ready, sums_added = sem("sums_ready"), sem("sums_added")
        more_offs, more_onehot, more_sums, more_added = sem("more_offs"), sem("more_onehot"), sem("more_sums"), sem("more_added")
        staged, agg_projected, rec_a, rec_ready = sem("staged"), sem("agg_projected"), sem("rec_a"), sem("rec_ready")
        u_ready, u_squares, u_var, u_std, u_root = sem("u_ready"), sem("u_squares"), sem("u_var"), sem("u_std"), sem("u_root")
        u_scaled, u_done, u_transposed, uT_ready = sem("u_scaled"), sem("u_done"), sem("u_transposed"), sem("uT_ready")
        out_projected, out_ready = sem("out_projected"), sem("out_ready")
        out_written = two("out_written")

        def in_pairs(eng, pairs, body, tail=()):
            body(0, 0, 0)
            body(1, 1, 0)
            with eng.Fori(1, pairs) as i:
                for b in range(2):
                    body(2 * i + b, b, i)
            for s in tail:
                body(s, s % 2, s // 2)

        def chunks(eng, body):
            in_pairs(eng, PAIRS, body, tail=(CHUNKS - 2, CHUNKS - 1))

        def groups(eng, body):
            in_pairs(eng, GROUPS // 2, body)

        def at_least(step, k):
            return step >= k if isinstance(step, int) else k <= 2

        def size_of(c):
            tail = isinstance(c, int) and c == CHUNKS - 1
            return (TAIL_ROWS, TAIL_SLOTS) if tail else (P, SLOTS)

        def packs_of(slots):
            return [(q, min(PACK, slots - q * PACK)) for q in range((slots + PACK - 1) // PACK)]

        def inverse_root(dve, var, std, r, a, b, seed, at):
            nc.vector.reciprocal(r, std).then_inc(seed, 1)
            dve.wait_ge(seed, at + 1)
            nc.vector.scalar_tensor_tensor(a, var, -0.5, r, ALU.mult, ALU.mult).then_inc(seed, 1)
            dve.wait_ge(seed, at + 2)
            nc.vector.tensor_tensor(b, a, r, ALU.mult).then_inc(seed, 1)
            dve.wait_ge(seed, at + 3)
            nc.vector.scalar_tensor_tensor(r, b, 1.5, r, ALU.add, ALU.mult).then_inc(seed, 1)
            dve.wait_ge(seed, at + 4)

        block = ctx.enter_context(nc.Block())

        @block.sync
        def _(sp):
            def load_x(g, b, n):
                if at_least(g, 2):
                    sp.wait_ge(x_loaded[b], 16 * n)
                sp.dma_start(res[:, bass.ds(g * GT, GT), :], x_v[:, bass.ds(g * GT, GT), :]).then_inc(x_loaded[b], 16)
            groups(sp, load_x)

            def store_table(g, b, n):
                if at_least(g, 2):
                    sp.wait_ge(table_written[b], 16 * n)
                sp.wait_ge(nodes_ready, g + 1)
                sp.dma_start(table_v[:, bass.ds(g * GT, GT), :],
                             nodes[:, bass.ds(g * GT, GT), 0:H]).then_inc(table_written[b], 16)
            for g in range(GROUPS):
                store_table(g, g % 2, g // 2)

            def load_edges(c, b, n):
                r, s = size_of(c)
                if r == P:
                    fs, ss, ds = edge_v[c, :, :], src_v[c, :, :], dst_v[c, :, :]
                else:
                    fs, ss, ds = edge_t, src_t, dst_t
                if at_least(c, 2):
                    sp.wait_ge(feat_transposed, c - 1)
                sp.dma_start(feat[b][0:r, 0:s * DE], fs).then_inc(feat_loaded[b], 16)
                if at_least(c, 2):
                    sp.wait_ge(offs_ready, c - 1)
                sp.dma_start(dsts[b][0:r, 0:s], ds).then_inc(dst_loaded[b], 16)
                if at_least(c, 2):
                    sp.wait_ge(gathered[b], 16 * SLOTS * n)
                sp.dma_start(srcs[b][0:r, 0:s], ss).then_inc(src_loaded[b], 16)
            chunks(sp, load_edges)

            def store_out(g, b, n):
                sp.wait_ge(out_ready, g + 1)
                sp.dma_start(out_v[:, bass.ds(g * GT, GT), :], o_t[b][:, :, :]).then_inc(out_written[b], 16)
            groups(sp, store_out)
            for b in range(2):
                sp.wait_ge(out_written[b], 16 * (GROUPS // 2))

        @block.gpsimd
        def _(pool):
            nc.gpsimd.memset(ident[:, :], 0.0).then_inc(ident_clear, 1)
            nc.gpsimd.memset(ones[:, :], 1.0).then_inc(ones_ready, 1)
            nc.gpsimd.iota(ramp_i[:, :], pattern=[[1, W]], base=0, channel_multiplier=0).then_inc(ramp_made, 1)
            pool.wait_ge(ident_clear, 1)
            nc.gpsimd.affine_select(out=ident[:, :], in_=ident[:, :], compare_op=ALU.not_equal, fill=1.0,
                                    base=0, pattern=[[-1, P]], channel_multiplier=1).then_inc(ident_ready, 1)

            def add_h(g, b, n):
                pool.wait_ge(h_ready, GT * (g + 1))
                xs = res[:, bass.ds(g * GT, GT), :].rearrange("p k f -> p (k f)")
                nc.gpsimd.tensor_tensor(xs, xs, h_t[b][:, :], ALU.add).then_inc(x_plus_h, 1)
            groups(pool, add_h)

            for b in range(2):
                pool.wait_ge(table_written[b], 16 * (GROUPS // 2))

            def gather(c, b, n):
                r, s = size_of(c)
                if at_least(c, 2):
                    pool.wait_ge(z_ready, c - 1)
                pool.wait_ge(src_loaded[b], 16 * (n + 1))
                pool.sem_inc(gather_begun, 1)
                for j in range(s):
                    nc.gpsimd.indirect_dma_start(
                        out=rows[b][0:r, j, :], out_offset=None, in_=table[:, :],
                        in_offset=bass.IndirectOffsetOnAxis(ap=srcs[b][0:r, j:j + 1], axis=0),
                    ).then_inc(gathered[b], 16)
            chunks(pool, gather)

            pool.wait_ge(sums_added, CHUNKS)

            def stage(g, b, n):
                if at_least(g, 2):
                    pool.wait_ge(agg_projected, g - 1)
                span = bass.ds(g * GT * NR, GT * NR)
                nc.gpsimd.tensor_copy(agg[b][:, :], acc[:, 0, span]).then_inc(staged, 1)
                nc.gpsimd.tensor_copy(cnt[b][:, :], acc[0:1, 1, span]).then_inc(staged, 1)
            groups(pool, stage)

        @block.tensor
        def _(pe):
            pe.wait_ge(ident_ready, 1)
            pe.wait_ge(cen_ready, 1)

            def project_nodes(g, b):
                pe.wait_ge(hT_ready, g + 1)
                if at_least(g, 2):
                    pe.wait_ge(nodes_ready, g - 1)
                for t in range(GT):
                    last = nc.tensor.matmul(ps_nodes[b][0:NR, t * 2 * H:(t + 1) * 2 * H], hT[b][:, t * P:t * P + NR],
                                            cen[:, CEN_E1:CEN_N1 + 1, :], start=True, stop=True)
                last.then_inc(projected, 1)

            def node_step(g, b, n):
                pe.wait_ge(h_ready, GT * (g + 1))
                if at_least(g, 1):
                    pe.wait_ge(hT_ready, g)
                for t in range(GT):
                    last = nc.tensor.transpose(ps_hT[:, t * P:t * P + NR], h_t[b][:, t * D:(t + 1) * D], ident[0:NR, 0:NR])
                last.then_inc(h_transposed, 1)
                if at_least(g, 1):
                    project_nodes(g - 1, 1 - b)
            groups(pe, node_step)
            project_nodes(GROUPS - 1, 1)

            pe.wait_ge(late_loaded, 16 * 7)
            pe.wait_ge(nodes_ready, GROUPS - 1)
            pe.wait_ge(prep, 2)
            nc.tensor.transpose(banks(2, P), we2[:, :], ident[:, :]).then_inc(pe_prep, 1)
            nc.tensor.matmul(banks(3, 1), we2[:, :], cols[:, 0:1], start=True, stop=True).then_inc(pe_prep, 1)
            nc.tensor.matmul(banks(4, D), last_b[:, :], wn2[:, :], start=True, stop=True).then_inc(pe_prep, 1)
            pe.wait_ge(prep, 4)
            pe.wait_ge(hT_ready, GROUPS)
            nc.tensor.matmul(banks(0, H), we2T[:, :], cen[:, CEN_N2, :], start=True, stop=True).then_inc(pe_prep, 1)
            nc.tensor.matmul(banks(1, H)[0:1, :], shift_col[:, :], cen[:, CEN_N2, :], start=True, stop=True).then_inc(pe_prep, 1)
            pe.wait_ge(prep, 6)
            pe.wait_ge(nodes_ready, GROUPS)
            nc.tensor.matmul(banks(5, 4 * HALF), ones[0:HALF, :], spread_diag[:, :, :, :].rearrange("p a b q -> p (a b q)"),
                             start=True, stop=True).then_inc(pe_prep, 1)
            pe.wait_ge(prep_ready, 1)

            windows = pe.alloc_register("pe_windows")
            pe.reg_mov(windows, 0)

            def window_sums(b, r, s, signal):
                for part, left in ((0, None), (1, ones)):
                    for j in range(s):
                        lhsT = z[b][0:r, j, :] if left is None else ones[0:r, :]
                        last = nc.tensor.matmul(ps_sum[b][:, part * W:(part + 1) * W], lhsT, onehot[b][0:r, j, :],
                                                start=(j == 0), stop=(j == s - 1))
                last.then_inc(signal, 1)

            def sum_messages(c, b):
                r, s = size_of(c)
                pe.wait_ge(message_ready, c + 1)
                pe.wait_ge(onehot_ready, c + 1)
                if at_least(c, 2):
                    pe.wait_ge(sums_added, c - 1)
                window_sums(b, r, s, sums_ready)
                more = pe.value_load(more_i[0:1, bass.ds(c, 1)], min_val=0, max_val=MOST)
                with pe.If(more > 0):
                    with pe.Fori(0, more):
                        pe.reg_add(windows, windows, 1)
                        pe.wait_ge(more_onehot, pe.snap(windows))
                        window_sums(b, r, s, more_sums)

            def edge_step(c, b, n):
                r, s = size_of(c)
                pe.wait_ge(feat_loaded[b], 16 * (n + 1))
                if at_least(c, 2):
                    pe.wait_ge(featT_ready, c - 1)
                for q, k in packs_of(s):
                    last = nc.tensor.transpose(ps_featT[b][0:k * DE, q * P:q * P + r],
                                               feat[b][0:r, q * P:q * P + k * DE], ident[0:r, 0:r])
                last.then_inc(feat_transposed, 1)
                pe.wait_ge(featT_ready, c + 1)
                if at_least(c, 2):
                    pe.wait_ge(z_ready, c - 1)
                for q, k in packs_of(s):
                    last = nc.tensor.matmul(ps_edge[b][0:r, q * PACK * H:(q * PACK + k) * H],
                                            featT[b][0:k * DE, q * P:q * P + r],
                                            wedge[0:k * DE, 0:k, :], start=True, stop=True)
                last.then_inc(edge_projected, 1)
                if at_least(c, 1):
                    sum_messages(c - 1, 1 - b)
            chunks(pe, edge_step)
            sum_messages(CHUNKS - 1, (CHUNKS - 1) % 2)

            def back_half(g, b):
                pe.wait_ge(u_done, g + 1)
                if at_least(g, 1):
                    pe.wait_ge(uT_ready, g)
                for t in range(GT):
                    last = nc.tensor.transpose(ps_uT[:, t * P:t * P + NR], u[b][:, t, :], ident[0:NR, 0:NR])
                last.then_inc(u_transposed, 1)
                pe.wait_ge(uT_ready, g + 1)
                if at_least(g, 1):
                    pe.wait_ge(out_ready, g)
                for t in range(GT):
                    last = nc.tensor.matmul(ps_out[0:NR, t * D:(t + 1) * D], uT[b][:, t * P:t * P + NR], wn2[:, :],
                                            start=True, stop=True)
                last.then_inc(out_projected, 1)

            def last_step(g, b, n):
                pe.wait_ge(staged, 2 * (g + 1))
                if at_least(g, 2):
                    pe.wait_ge(u_ready, GT * (g - 1))
                for t in range(GT):
                    tile = slice(t * NR, (t + 1) * NR)
                    nc.tensor.matmul(ps_agg[b][0:NR, t * H:(t + 1) * H], agg[b][:, tile], fused[:, :], start=True, stop=False)
                    nc.tensor.matmul(ps_agg[b][0:NR, t * H:(t + 1) * H], cnt[b][:, tile], shift_row[:, :], start=False, stop=True)
                for t in range(GT):
                    tile = slice(t * NR, (t + 1) * NR)
                    last = nc.tensor.matmul(ps_agg[b][0:NR, GT * H + t:GT * H + t + 1], cnt[b][:, tile], ones[0:1, 0:1],
                                            start=True, stop=True)
                last.then_inc(agg_projected, 1)
                if at_least(g, 1):
                    back_half(g - 1, 1 - b)
            groups(pe, last_step)
            back_half(GROUPS - 1, 1)

        @block.scalar
        def _(act):
            def spread(v):
                return v.unsqueeze(0).to_broadcast([P, H])
            for slot, w in ((CEN_E1, We1[0:D, :]), (CEN_N1, Wn1[0:D, :]), (CEN_BE1, spread(be1)), (CEN_BN1, spread(bn1)),
                            (CEN_N2, Wn1[D:D + H, :])):
                act.dma_start(cen[:, slot, :], w).then_inc(w_loaded, 16)
            for q in range(PACK):
                act.dma_start(cen[q * DE:(q + 1) * DE, CEN_EDGE, :], We1[D:D + DE, :]).then_inc(w_loaded, 16)
            act.dma_start(ends[0:HALF - 1, :, :], dst[0:(HALF - 1) * 2 * CHUNK].rearrange("(q c e) -> q c e", c=2, e=CHUNK)
                          ).then_inc(ends_loaded, 16)
            act.dma_start(ends[HALF - 1:HALF, 0, :], dst[(FULL - 1) * CHUNK:FULL * CHUNK].unsqueeze(0)).then_inc(ends_loaded, 16)
            act.dma_start(ends[HALF - 1:HALF, 1, :], dst[E - CHUNK:E].unsqueeze(0)).then_inc(ends_loaded, 16)
            for slot, w in ((V_GE, ge1), (V_BE, ble1), (V_GN, gn1), (V_BN, bln1), (V_BO, bn2)):
                act.dma_start(vec[:, slot, :], spread(w)).then_inc(late_loaded, 16)
            act.dma_start(we2[:, :], We2).then_inc(late_loaded, 16)
            act.dma_start(wn2[:, :], Wn2).then_inc(late_loaded, 16)
            for k, v in enumerate((ble1, be2, bln1)):
                act.dma_start(cols[:, k:k + 1], v.unsqueeze(1)).then_inc(cols_loaded, 16)

            def copy_hT(g, b):
                act.wait_ge(h_transposed, g + 1)
                if at_least(g, 2):
                    act.wait_ge(projected, g - 1)
                w = (GT - 1) * P + NR
                src_ = ps_hT[:, :].rearrange("p (t c) -> p t c", c=P)[:, :, 0:NR]
                dst_ = hT[b][:, :].rearrange("p (t c) -> p t c", c=P)[:, :, 0:NR]
                nc.scalar.copy(dst_, src_).then_inc(hT_ready, 1)

            def node_step(g, b, n):
                act.wait_ge(nvar_ready, g + 1)
                nc.scalar.activation(small[b][0:NR, S_STD, 0:GT], small[b][0:NR, S_VAR, 0:GT], ACT.Sqrt).then_inc(nstd_ready, 1)
                if at_least(g, 1):
                    copy_hT(g - 1, 1 - b)
                act.wait_ge(norm_ready, g + 1)
                if at_least(g, 2):
                    act.wait_ge(x_plus_h, g - 1)
                for t in range(GT):
                    nc.scalar.activation(h_t[b][:, t * D:(t + 1) * D], res[:, g * GT + t, :], ACT.Relu,
                                         bias=small[b][0:NR, S_NMR, t:t + 1], scale=small[b][0:NR, S_R, t:t + 1],
                                         ).then_inc(h_ready, 1)
            groups(act, node_step)
            copy_hT(GROUPS - 1, 1)

            def edge_step(c, b, n):
                r, s = size_of(c)
                act.wait_ge(feat_transposed, c + 1)
                if at_least(c, 2):
                    act.wait_ge(edge_projected, c - 1)
                if r == P:
                    nc.scalar.copy(featT[b][:, :], ps_featT[b][:, :]).then_inc(featT_ready, 1)
                else:
                    for q, k in packs_of(s):
                        last = nc.scalar.copy(featT[b][0:k * DE, q * P:q * P + r], ps_featT[b][0:k * DE, q * P:q * P + r])
                    last.then_inc(featT_ready, 1)
                act.wait_ge(z_ready, c + 1)
                if at_least(c, 2):
                    act.wait_ge(var_ready, c - 1)
                for j in range(s):
                    last = nc.scalar.activation(trash[0:r, j, :], z[b][0:r, j, :], ACT.Square, accum_out=squares[b][0:r, j:j + 1])
                last.then_inc(squares_done, 1)
                act.wait_ge(var_ready, c + 1)
                nc.scalar.activation(small[b][0:r, S_STD, 0:s], small[b][0:r, S_VAR, 0:s], ACT.Sqrt).then_inc(std_ready, 1)
            chunks(act, edge_step)

            def copy_uT(g, b):
                act.wait_ge(u_transposed, g + 1)
                if at_least(g, 2):
                    act.wait_ge(out_projected, g - 1)
                src_ = ps_uT[:, :].rearrange("p (t c) -> p t c", c=P)[:, :, 0:NR]
                dst_ = uT[b][:, :].rearrange("p (t c) -> p t c", c=P)[:, :, 0:NR]
                nc.scalar.copy(dst_, src_).then_inc(uT_ready, 1)

            def last_step(g, b, n):
                for t in range(GT):
                    act.wait_ge(u_ready, GT * g + t + 1)
                    last = nc.scalar.activation(trash[0:NR, t, :], u[b][:, t, :], ACT.Square, accum_out=squares[b][0:NR, t:t + 1])
                last.then_inc(u_squares, 1)
                act.wait_ge(u_var, g + 1)
                nc.scalar.activation(small[b][0:NR, S_STD, 0:GT], small[b][0:NR, S_VAR, 0:GT], ACT.Sqrt).then_inc(u_std, 1)
                if at_least(g, 1):
                    copy_uT(g - 1, 1 - b)
            groups(act, last_step)
            copy_uT(GROUPS - 1, 1)

        @block.vector
        def _(dve):
            dve.wait_ge(w_loaded, 16 * (5 + PACK))
            nc.vector.tensor_reduce(cen_mean[:, :], cen[:, :, :], AX.X, ALU.add).then_inc(cen_step, 1)
            dve.wait_ge(cen_step, 1)
            nc.vector.tensor_scalar(cen_mean[:, :], cen_mean[:, :], 1.0 / H, None, ALU.mult).then_inc(cen_step, 1)
            dve.wait_ge(cen_step, 2)
            nc.vector.tensor_tensor(cen[:, :, :], cen[:, :, :], cen_mean[:, :].unsqueeze(2).to_broadcast([P, 6, H]),
                                    ALU.subtract).then_inc(cen_ready, 1)

            def keep_nodes(g, b):
                dve.wait_ge(projected, g + 1)
                nc.vector.tensor_tensor(nodes[:, bass.ds(g * GT, GT), :],
                                        ps_nodes[b][0:NR, 0:GT * 2 * H].rearrange("p (t c) -> p t c", t=GT),
                                        cen[0:NR, CEN_BE1:CEN_BN1 + 1, :].rearrange("p a c -> p (a c)").unsqueeze(1).to_broadcast([NR, GT, 2 * H]),
                                        ALU.add).then_inc(nodes_ready, 1)

            dve.wait_ge(cen_ready, 1)

            def node_step(g, b, n):
                dve.wait_ge(x_loaded[b], 16 * (n + 1))
                for t in range(GT):
                    last = nc.vector.bn_stats(bn[b][:, t, :], res[:, g * GT + t, :])
                last.then_inc(bn_done, 1)
                dve.wait_ge(bn_done, g + 1)
                dve.sem_inc(bn_seen, 1)
                for t in range(GT):
                    last = nc.vector.bn_aggr(mv[b][:, t, :], bn[b][:, t, :])
                last.then_inc(aggr_done, 1)
                dve.wait_ge(aggr_done, g + 1)
                v, sd, r, a, q, nmr = (small[b][0:NR, k, 0:GT] for k in range(6))
                if at_least(g, 2):
                    dve.wait_ge(h_ready, GT * (g - 1))
                nc.vector.tensor_scalar(v, mv[b][:, :, 1], EPS_X, None, ALU.add).then_inc(nvar_ready, 1)
                dve.wait_ge(nstd_ready, g + 1)
                inverse_root(dve, v, sd, r, a, q, nroot, 4 * g)
                nc.vector.scalar_tensor_tensor(nmr, mv[b][:, :, 0], -1.0, r, ALU.mult, ALU.mult).then_inc(norm_ready, 1)
                if at_least(g, 1):
                    keep_nodes(g - 1, 1 - b)
            groups(dve, node_step)

            nc.vector.memset(wedge[:, :, :], 0.0).then_inc(prep, 1)
            dve.wait_ge(cols_loaded, 16 * 3)
            nc.vector.tensor_copy(last_b[:, :], cols[:, 2:3].to_broadcast([P, P])).then_inc(prep, 1)
            keep_nodes(GROUPS - 1, 1)
            dve.wait_ge(pe_prep, 1)
            nc.vector.tensor_copy(we2T[:, :], banks(2, P)).then_inc(prep, 1)
            dve.wait_ge(pe_prep, 2)
            nc.vector.tensor_tensor(shift_col[:, :], banks(3, 1), cols[:, 1:2], ALU.add).then_inc(prep, 1)
            dve.wait_ge(ends_loaded, 16 * 3)
            for k, op in enumerate((ALU.min, ALU.max)):
                last = nc.vector.tensor_reduce(lohi[:, k, :], ends[:, :, :], AX.X, op)
            last.then_inc(prep, 1)
            dve.wait_ge(prep, 5)
            for k in range(2):
                for c in range(2):
                    last = nc.vector.tensor_scalar(spread_diag[:, k, c, :], ident[0:HALF, 0:HALF], lohi[:, k, c:c + 1], None, ALU.mult)
            last.then_inc(prep, 1)
            dve.wait_ge(late_loaded, 16 * 7)
            nc.vector.tensor_scalar(neg[:, 0, :], vec[:, V_BE, :], -1.0, None, ALU.mult).then_inc(prep, 1)
            nc.vector.tensor_scalar(neg[:, 1, :], vec[:, V_BN, :], -1.0, None, ALU.mult).then_inc(prep, 1)
            dve.wait_ge(ramp_made, 1)
            nc.vector.tensor_copy(ramp[:, :], ramp_i[:, :]).then_inc(ramp_ready, 1)
            for q in range(PACK):
                nc.vector.tensor_copy(wedge[q * DE:(q + 1) * DE, q, :], cen[q * DE:(q + 1) * DE, CEN_EDGE, :]).then_inc(prep, 1)
            dve.wait_ge(pe_prep, 3)
            nc.vector.tensor_tensor(last_bias[:, :], banks(4, D), vec[:, V_BO, :], ALU.add).then_inc(prep, 1)
            dve.wait_ge(pe_prep, 4)
            nc.vector.tensor_copy(fused[:, :], banks(0, H)).then_inc(prep, 1)
            dve.wait_ge(pe_prep, 5)
            nc.vector.tensor_copy(shift_row[:, :], banks(1, H)[0:1, :]).then_inc(prep, 1)
            dve.wait_ge(pe_prep, 6)
            bounds = banks(5, 4 * HALF).rearrange("p (k c q) -> p k q c", k=2, c=2)
            nc.vector.tensor_copy(base[:, :].rearrange("p (q c) -> p q c", c=2), bounds[:, 0, :, :]).then_inc(prep, 1)
            n_prep = 2 + 4 + 2 + PACK + 4
            dve.wait_ge(prep, n_prep)
            nc.vector.tensor_copy(base_i[:, :], base[0:1, :])
            nc.vector.tensor_tensor(reach[:, :].rearrange("p (q c) -> p q c", c=2), bounds[0:1, 1, :, :],
                                    base[0:1, :].rearrange("p (q c) -> p q c", c=2), ALU.subtract).then_inc(prep, 1)
            dve.wait_ge(prep, n_prep + 1)
            nc.vector.tensor_copy(reach_i[:, :], reach[:, :]).then_inc(prep, 1)
            dve.wait_ge(prep, n_prep + 2)
            nc.vector.tensor_scalar(more_i[:, :], reach_i[:, :], SHIFT, None, ALU.arith_shift_right).then_inc(prep_ready, 1)
            nc.vector.memset(acc[:, :, :], 0.0).then_inc(sums_cleared, 1)
            dve.wait_ge(x_plus_h, GROUPS)
            nc.vector.tensor_tensor(res[:, :, :], res[:, :, :], last_bias[0:NR, :].unsqueeze(1).to_broadcast([NR, TILES, D]),
                                    ALU.add).then_inc(res_ready, 1)
            dve.wait_ge(prep_ready, 1)
            dve.wait_ge(ramp_ready, 1)
            dve.wait_ge(sums_cleared, 1)

            windows = dve.alloc_register("dve_windows")
            dve.reg_mov(windows, 0)

            def make_onehot(b, r, s, signal):
                nc.vector.tensor_tensor(onehot[b][0:r, 0:s, :], ramp[0:r, :].unsqueeze(1).to_broadcast([r, s, W]),
                                        offs[b][0:r, 0:s].unsqueeze(2).to_broadcast([r, s, W]), ALU.is_equal).then_inc(signal, 1)

            def add_sums(c, b):
                r, s = size_of(c)
                dve.wait_ge(sums_ready, c + 1)
                if at_least(c, 1):
                    dve.wait_ge(sums_added, c)
                start = dve.value_load(base_i[0:1, bass.ds(c, 1)], min_val=0, max_val=N - 1)
                more = dve.value_load(more_i[0:1, bass.ds(c, 1)], min_val=0, max_val=MOST)
                window = acc[:, :, bass.ds(start, W)]
                sums = ps_sum[b][:, :].rearrange("p (k w) -> p k w", k=2)
                nc.vector.tensor_tensor(window, window, sums, ALU.add).then_inc(sums_added, 1)
                with dve.If(more > 0):
                    with dve.Fori(1, more + 1) as k:
                        dve.reg_add(windows, windows, 1)
                        w = dve.snap(windows)
                        dve.wait_ge(sums_added, c + 1)
                        nc.vector.tensor_scalar(offs[b][0:r, 0:s], offs[b][0:r, 0:s], -float(W), None, ALU.add).then_inc(more_offs, 1)
                        dve.wait_ge(more_offs, w)
                        make_onehot(b, r, s, more_onehot)
                        dve.wait_ge(more_sums, w)
                        far = nc.s_assert_within(start + k * W, 0, N - 1)
                        window = acc[:, :, bass.ds(far, W)]
                        nc.vector.tensor_tensor(window, window, sums, ALU.add).then_inc(more_added, 1)
                        dve.wait_ge(more_added, w)

            def edge_step(c, b, n):
                r, s = size_of(c)
                dve.wait_ge(dst_loaded[b], 16 * (n + 1))
                nc.vector.tensor_scalar(offs[b][0:r, 0:s], dsts[b][0:r, 0:s], base[0:r, bass.ds(c, 1)], None, ALU.subtract
                                        ).then_inc(offs_ready, 1)
                dve.wait_ge(offs_ready, c + 1)
                make_onehot(b, r, s, onehot_ready)
                dve.wait_ge(gathered[b], 16 * SLOTS * n + 16 * s)
                dve.wait_ge(edge_projected, c + 1)
                nc.vector.tensor_tensor(z[b][0:r, 0:s, :], rows[b][0:r, 0:s, :],
                                        ps_edge[b][0:r, 0:s * H].rearrange("p (s h) -> p s h", s=s), ALU.add).then_inc(z_ready, 1)
                if at_least(c, 1):
                    add_sums(c - 1, 1 - b)
                v, sd, rs, a, q = (small[b][0:r, k, 0:s] for k in range(5))
                dve.wait_ge(squares_done, c + 1)
                nc.vector.tensor_scalar(v, squares[b][0:r, 0:s], 1.0 / H, EPS_MLP, ALU.mult, ALU.add).then_inc(var_ready, 1)
                dve.wait_ge(std_ready, c + 1)
                inverse_root(dve, v, sd, rs, a, q, root, 4 * c)
                for j in range(s):
                    last = nc.vector.scalar_tensor_tensor(z[b][0:r, j, :], z[b][0:r, j, :], rs[:, j:j + 1], vec[0:r, V_GE, :],
                                                          ALU.mult, ALU.mult)
                last.then_inc(scaled, 1)
                dve.wait_ge(scaled, c + 1)
                nc.vector.tensor_tensor(z[b][0:r, 0:s, :], z[b][0:r, 0:s, :],
                                        neg[0:r, 0, :].unsqueeze(1).to_broadcast([r, s, H]), ALU.max).then_inc(message_ready, 1)
            chunks(dve, edge_step)
            add_sums(CHUNKS - 1, (CHUNKS - 1) % 2)

            dve.wait_ge(res_ready, 1)

            def add_residual(g, b, n):
                dve.wait_ge(out_projected, g + 1)
                if at_least(g, 2):
                    dve.wait_ge(out_written[b], 16 * n)
                nc.vector.tensor_tensor(o_t[b][:, :, :], ps_out[0:NR, :].rearrange("p (t c) -> p t c", t=GT),
                                        res[:, bass.ds(g * GT, GT), :], ALU.add).then_inc(out_ready, 1)

            def last_step(g, b, n):
                v, sd, rs, a, q, rec = (small[b][0:NR, k, 0:GT] for k in range(6))
                dve.wait_ge(agg_projected, g + 1)
                nc.vector.tensor_scalar(a, ps_agg[b][0:NR, GT * H:GT * H + GT], 1.0, None, ALU.max).then_inc(rec_a, 1)
                dve.wait_ge(rec_a, g + 1)
                nc.vector.reciprocal(rec, a).then_inc(rec_ready, 1)
                dve.wait_ge(rec_ready, g + 1)
                if at_least(g, 2):
                    dve.wait_ge(u_transposed, g - 1)
                for t in range(GT):
                    nc.vector.scalar_tensor_tensor(u[b][:, t, :], ps_agg[b][0:NR, t * H:(t + 1) * H], rec[:, t:t + 1],
                                                   nodes[:, g * GT + t, H:2 * H], ALU.mult, ALU.add).then_inc(u_ready, 1)
                dve.wait_ge(u_squares, g + 1)
                nc.vector.tensor_scalar(v, squares[b][0:NR, 0:GT], 1.0 / H, EPS_MLP, ALU.mult, ALU.add).then_inc(u_var, 1)
                dve.wait_ge(u_std, g + 1)
                inverse_root(dve, v, sd, rs, a, q, u_root, 4 * g)
                for t in range(GT):
                    last = nc.vector.scalar_tensor_tensor(u[b][:, t, :], u[b][:, t, :], rs[:, t:t + 1], vec[0:NR, V_GN, :],
                                                          ALU.mult, ALU.mult)
                last.then_inc(u_scaled, 1)
                dve.wait_ge(u_scaled, g + 1)
                nc.vector.tensor_tensor(u[b][:, :, :], u[b][:, :, :], neg[0:NR, 1, :].unsqueeze(1).to_broadcast([NR, GT, H]),
                                        ALU.max).then_inc(u_done, 1)
                if at_least(g, 1):
                    add_residual(g - 1, 1 - b, n if b == 1 else n - 1)
            groups(dve, last_step)
            add_residual(GROUPS - 1, 1, GROUPS // 2 - 1)


_INS = ["x", "src", "dst", "edge_attr_32", "L0_gnn_We1", "L0_gnn_be1", "L0_gnn_ge1", "L0_gnn_ble1", "L0_gnn_We2", "L0_gnn_be2",
        "L0_gnn_Wn1", "L0_gnn_bn1", "L0_gnn_gn1", "L0_gnn_bln1", "L0_gnn_Wn2", "L0_gnn_bn2"]


def kernel(**inputs):
    import numpy as _np
    import concourse.bacc as _bacc
    from concourse import mybir as _mybir
    from concourse.bass_utils import run_bass_kernel_spmd as _run

    nc = _bacc.Bacc("TRN2", target_bir_lowering=False, num_devices=1)
    arrays, args = {}, []
    for name in _INS:
        a = _np.ascontiguousarray(inputs[name])
        arrays[f"in_{name}_dram"] = a
        args.append(nc.dram_tensor(f"in_{name}_dram", a.shape, _mybir.dt.from_np(a.dtype), kind="ExternalInput").ap())
    x = inputs["x"]
    args.append(nc.dram_tensor("out_0_dram", x.shape, _mybir.dt.from_np(_np.dtype(x.dtype)), kind="ExternalOutput").ap())
    graph_layer(nc, *args)
    r = _run(nc, [arrays], core_ids=[0])
    return r.results[0]["out_0_dram"]
```

```python
import concourse.bass as bass
from concourse import mybir
from contextlib import ExitStack


def graph_layer(nc, x, src, dst, edge, We1, be1, ge1, ble1, We2, be2, Wn1, bn1, gn1, bln1, Wn2, bn2, out):
    fp32 = mybir.dt.float32
    bf16 = mybir.dt.bfloat16
    i32 = mybir.dt.int32
    ALU = mybir.AluOpType
    ACT = mybir.ActivationFunctionType
    AX = mybir.AxisListType

    N, D = x.shape
    E, DE = edge.shape
    H = We2.shape[0]
    P = 128
    EPS_X = 1e-5
    EPS_MLP = 1e-6
    assert D == H == P

    SLOTS = 8
    CHUNK = P * SLOTS
    FULL = E // CHUNK
    TAIL = E - FULL * CHUNK
    TAIL_SLOTS = next(s for s in range(1, SLOTS + 1) if TAIL % s == 0 and TAIL // s <= P)
    TAIL_ROWS = TAIL // TAIL_SLOTS
    PAIRS = FULL // 2
    assert FULL % 2 == 1 and TAIL > 0
    CHUNKS = FULL + 1
    HALF = CHUNKS // 2
    W = 128
    SHIFT = W.bit_length() - 1
    MOST = (N - 1) // W
    PACK = P // DE
    PACKS = SLOTS // PACK

    NR = 125
    TILES = N // NR
    GT = 5
    GROUPS = TILES // GT
    assert TILES * NR == N and GROUPS * GT == TILES and GROUPS % 2 == 0
    GW = GT * D

    table = nc.dram_tensor("sender_table", (N, H), fp32).ap()
    x_v = x.rearrange("(k p) f -> p k f", p=NR)
    out_v = out.rearrange("(k p) f -> p k f", p=NR)
    table_v = table.rearrange("(k p) f -> p k f", p=NR)
    edge_v = edge[0:FULL * CHUNK, :].rearrange("(c p j) f -> c p (j f)", p=P, j=SLOTS)
    src_v = src[0:FULL * CHUNK].rearrange("(c p j) -> c p j", p=P, j=SLOTS)
    dst_v = dst[0:FULL * CHUNK].rearrange("(c p j) -> c p j", p=P, j=SLOTS)
    edge_t = edge[FULL * CHUNK:E, :].rearrange("(p j) f -> p (j f)", j=TAIL_SLOTS)
    src_t = src[FULL * CHUNK:E].rearrange("(p j) -> p j", j=TAIL_SLOTS)
    dst_t = dst[FULL * CHUNK:E].rearrange("(p j) -> p j", j=TAIL_SLOTS)

    ctx = ExitStack()
    with ctx:
        def sb(name, shape, dt=fp32):
            return ctx.enter_context(nc.sbuf_tensor(name, shape, dt))

        def sem(name):
            return ctx.enter_context(nc.semaphore(name))

        def two(name):
            return [sem(f"{name}{b}") for b in range(2)]

        acc = sb("acc", [P, 2, N + W])
        res = sb("res", [NR, TILES, D])
        nodes = sb("nodes", [NR, TILES, 2 * H])
        cen = sb("cen", [P, 6, H])
        CEN_E1, CEN_N1, CEN_BE1, CEN_BN1, CEN_N2, CEN_EDGE = range(6)
        cen_mean = sb("cen_mean", [P, 6])
        vec = sb("vec", [P, 3, H])
        V_GE, V_BE, V_BO = range(3)
        neg = sb("neg", [P, H])
        cols = sb("cols", [P, 4])
        we2 = sb("we2", [P, H])
        wn2 = sb("wn2", [P, D])
        we2T = sb("we2T", [P, H])
        fused = sb("fused", [P, H])
        shift_cols = sb("shift_cols", [P, P])
        shift = sb("shift", [P, H])
        eps = sb("eps", [P, 2])
        wedge = sb("wedge", [P, PACK, H])
        ident = sb("ident", [P, P])
        ones = sb("ones", [P, P])
        warm = sb("warm", [1, 1])
        ones_bf = sb("ones_bf", [P, P], bf16)
        ramp_i = sb("ramp_i", [P, W], i32)
        ramp = sb("ramp", [P, W])

        lohi = sb("lohi", [HALF, 2, 2])
        spread_diag = sb("spread_diag", [HALF, 2, 2, HALF])
        base = sb("base", [P, CHUNKS])
        base_i = sb("base_i", [1, CHUNKS], i32)
        reach = sb("reach", [1, CHUNKS])
        more_i = sb("more_i", [1, CHUNKS], i32)
        reach_i = sb("reach_i", [1, CHUNKS], i32)

        h_t = [sb(f"h_t{b}", [NR, GW]) for b in range(2)]
        hT = [sb(f"hT{b}", [P, GW]) for b in range(2)]
        bn = [sb(f"bn{b}", [NR, GT, 6]) for b in range(2)]
        mv = [sb(f"mv{b}", [NR, GT, 2]) for b in range(2)]
        small = [sb(f"small{b}", [P, 6, SLOTS]) for b in range(2)]
        S_VAR, S_STD, S_R, S_A, S_B, S_NMR = range(6)

        srcs = [sb(f"srcs{b}", [P, SLOTS], i32) for b in range(2)]
        dsts = [sb(f"dsts{b}", [P, SLOTS], i32) for b in range(2)]
        feat = [sb(f"feat{b}", [P, SLOTS * DE]) for b in range(2)]
        featT = [sb(f"featT{b}", [P, PACKS * P]) for b in range(2)]
        rows = [sb(f"rows{b}", [P, SLOTS, H]) for b in range(2)]
        z_two = sb("z_two", [P, 2, SLOTS, H])
        z = [z_two[:, b, :, :] for b in range(2)]
        ends = z_two[0:HALF, :, :, :].rearrange("q b s h -> q b (s h)").bitcast(i32)
        msg = [sb(f"msg{b}", [P, SLOTS, H]) for b in range(2)]
        offs = [sb(f"offs{b}", [P, SLOTS]) for b in range(2)]
        onehot = [sb(f"onehot{b}", [P, SLOTS, W]) for b in range(2)]
        onehot_bf = [sb(f"onehot_bf{b}", [P, SLOTS, W], bf16) for b in range(2)]
        squares = [sb(f"squares{b}", [P, SLOTS]) for b in range(2)]
        trash = sb("trash", [P, SLOTS, H], bf16)

        cnt_tiles = sb("cnt_tiles", [TILES, NR])
        recip = sb("recip", [NR, TILES])
        any_in = sb("any_in", [NR, TILES])
        agg = [rows[b][:, :, :].rearrange("p s h -> p (s h)")[:, 0:GT * NR] for b in range(2)]
        own_shift = onehot[0][0:NR, 0:GT, :]
        u = [z[b][0:NR, 0:GT, :] for b in range(2)]
        uT = hT
        o_t = [h_t[b][:, :].rearrange("p (t c) -> p t c", t=GT) for b in range(2)]

        ps = ctx.enter_context(nc.psum_tensor("ps", [P, 8, 512], fp32))
        flat = ps[:, :, :].rearrange("p b c -> p (b c)")

        def banks(first, width, rows=P):
            return flat[0:rows, 512 * first:512 * first + width]

        ps_hT = banks(0, GW)
        ps_nodes = [banks(2 + 3 * b, 3 * 512) for b in range(2)]
        ps_edge = [banks(2 * b, SLOTS * H) for b in range(2)]
        ps_featT = [banks(4 + b, PACKS * P) for b in range(2)]
        ps_sum = [banks(6 + b, 2 * W) for b in range(2)]
        ps_agg = [banks(2 * b, 1024) for b in range(2)]
        ps_cnt = banks(0, 768 + TILES, NR)[:, 768:]
        ps_uT = banks(4, GW)
        ps_out = banks(6, GW)

        w_loaded = sem("w_loaded")
        low_loaded = sem("low_loaded")
        late_loaded = sem("late_loaded")
        ends_loaded = sem("ends_loaded")
        ident_clear, ident_ready, const_ready = sem("ident_clear"), sem("ident_ready"), sem("const_ready")
        ramp_made, sums_cleared, wedge_clear = sem("ramp_made"), sem("sums_cleared"), sem("wedge_clear")
        cen_step, cen_ready = sem("cen_step"), sem("cen_ready")
        low_step, low_ready = sem("low_step"), sem("low_ready")
        prep = sem("prep")
        pe_prep = sem("pe_prep")
        prep_ready = sem("prep_ready")
        x_loaded = two("x_loaded")
        bn_done, bn_seen, aggr_done = sem("bn_done"), sem("bn_seen"), sem("aggr_done")
        nvar_ready, nstd_ready = sem("nvar_ready"), sem("nstd_ready")
        nroot = sem("nroot")
        norm_ready = sem("norm_ready")
        h_ready, h_transposed, hT_ready = sem("h_ready"), sem("h_transposed"), sem("hT_ready")
        projected = sem("projected")
        table_ready, own_kept, own_ready = sem("table_ready"), sem("own_kept"), sem("own_ready")
        x_plus_h = sem("x_plus_h")
        table_written = two("table_written")
        feat_loaded, src_loaded, dst_loaded = two("feat_loaded"), two("src_loaded"), two("dst_loaded")
        gathered = two("gathered")
        gather_begun = sem("gather_begun")
        feat_transposed, featT_ready, edge_projected = sem("feat_transposed"), sem("featT_ready"), sem("edge_projected")
        offs_ready, onehot_ready, onehot_bf_ready = sem("offs_ready"), sem("onehot_ready"), sem("onehot_bf_ready")
        z_ready, squares_done, var_ready, std_ready = sem("z_ready"), sem("squares_done"), sem("var_ready"), sem("std_ready")
        root = sem("root")
        scaled, message_ready = sem("scaled"), sem("message_ready")
        sums_ready, sums_added = sem("sums_ready"), sem("sums_added")
        more_offs, more_onehot, more_sums, more_added = sem("more_offs"), sem("more_onehot"), sem("more_sums"), sem("more_added")
        cnt_moved, cnt_turned, cnt_one, recip_ready = sem("cnt_moved"), sem("cnt_turned"), sem("cnt_one"), sem("recip_ready")
        any_ready, shift_made, own_full = sem("any_ready"), sem("shift_made"), sem("own_full")
        act_warm = sem("act_warm")
        res_ready, staged, agg_projected = sem("res_ready"), sem("staged"), sem("agg_projected")
        u_ready, u_squares, u_var, u_std = sem("u_ready"), sem("u_squares"), sem("u_var"), sem("u_std")
        u_root = sem("u_root")
        u_done, u_transposed, uT_ready = sem("u_done"), sem("u_transposed"), sem("uT_ready")
        out_projected, out_ready = sem("out_projected"), sem("out_ready")
        out_written = two("out_written")

        def in_pairs(eng, pairs, body, tail):
            for s in range(4):
                body(s, s % 2, s // 2)
            with eng.Fori(2, pairs) as i:
                for b in range(2):
                    body(2 * i + b, b, i)
            for s in tail:
                body(s, s % 2, s // 2)

        def chunks(eng, body):
            in_pairs(eng, PAIRS, body, tail=(CHUNKS - 2, CHUNKS - 1))

        def groups(eng, body):
            in_pairs(eng, GROUPS // 2 - 1, body, tail=(GROUPS - 2, GROUPS - 1))

        def at_least(step, k):
            return (step if isinstance(step, int) else step.min_val) >= k

        def size_of(c):
            tail = isinstance(c, int) and c == CHUNKS - 1
            return (TAIL_ROWS, TAIL_SLOTS) if tail else (P, SLOTS)

        def packs_of(slots):
            return [(q, min(PACK, slots - q * PACK)) for q in range((slots + PACK - 1) // PACK)]

        def inverse_root(dve, var, std, r, a, b, done, at):
            nc.vector.reciprocal(r, std).then_inc(done, 1)
            dve.wait_ge(done, at + 1)
            nc.vector.scalar_tensor_tensor(a, var, -0.5, r, ALU.mult, ALU.mult).then_inc(done, 1)
            dve.wait_ge(done, at + 2)
            nc.vector.tensor_tensor(b, a, r, ALU.mult).then_inc(done, 1)
            dve.wait_ge(done, at + 3)
            nc.vector.scalar_tensor_tensor(r, b, 1.5, r, ALU.add, ALU.mult).then_inc(done, 1)
            dve.wait_ge(done, at + 4)

        def spread(v):
            return v.unsqueeze(0).to_broadcast([P, H])

        block = ctx.enter_context(nc.Block())

        @block.sync
        def _(sp):
            def load_x(g, b, n):
                if at_least(g, 2):
                    sp.wait_ge(x_loaded[b], 16 * n)
                sp.dma_start(res[:, bass.ds(g * GT, GT), :], x_v[:, bass.ds(g * GT, GT), :]).then_inc(x_loaded[b], 16)
                if isinstance(g, int) and g == 1:
                    for slot, w in ((CEN_E1, We1[0:D, :]), (CEN_N1, Wn1[0:D, :]), (CEN_BE1, spread(be1)), (CEN_BN1, spread(bn1))):
                        sp.dma_start(cen[:, slot, :], w).then_inc(w_loaded, 16)
            groups(sp, load_x)

            sp.dma_start(ends[0:HALF - 1, :, :], dst[0:(HALF - 1) * 2 * CHUNK].rearrange("(q c e) -> q c e", c=2, e=CHUNK)
                         ).then_inc(ends_loaded, 16)
            sp.dma_start(ends[HALF - 1:HALF, 0, :], dst[(FULL - 1) * CHUNK:FULL * CHUNK].unsqueeze(0)).then_inc(ends_loaded, 16)
            sp.dma_start(ends[HALF - 1:HALF, 1, :], dst[E - CHUNK:E].unsqueeze(0)).then_inc(ends_loaded, 16)
            for slot, w in ((V_GE, ge1), (V_BE, ble1), (V_BO, bn2)):
                sp.dma_start(vec[:, slot, :], spread(w)).then_inc(late_loaded, 16)
            sp.dma_start(we2[:, :], We2).then_inc(late_loaded, 16)
            sp.dma_start(wn2[:, :], Wn2).then_inc(late_loaded, 16)
            for k, v in enumerate((ble1, be2, gn1, bln1)):
                sp.dma_start(cols[:, k:k + 1], v.unsqueeze(1)).then_inc(late_loaded, 16)

            for g in range(GROUPS):
                if g >= 2:
                    sp.wait_ge(table_written[g % 2], 16 * (g // 2))
                sp.wait_ge(table_ready, g + 1)
                sp.dma_start(table_v[:, g * GT:(g + 1) * GT, :], nodes[:, g * GT:(g + 1) * GT, 0:H]).then_inc(table_written[g % 2], 16)

            def load_edges(c, b, n):
                r, s = size_of(c)
                if r == P:
                    fs, ss, ds = edge_v[c, :, :], src_v[c, :, :], dst_v[c, :, :]
                else:
                    fs, ss, ds = edge_t, src_t, dst_t
                if at_least(c, 2):
                    sp.wait_ge(feat_transposed, c - 1)
                sp.dma_start(feat[b][0:r, 0:s * DE], fs).then_inc(feat_loaded[b], 16)
                if at_least(c, 2):
                    sp.wait_ge(gathered[b], 16 * SLOTS * n)
                sp.dma_start(srcs[b][0:r, 0:s], ss).then_inc(src_loaded[b], 16)
                if at_least(c, 2):
                    sp.wait_ge(offs_ready, c - 1)
                sp.dma_start(dsts[b][0:r, 0:s], ds).then_inc(dst_loaded[b], 16)
            chunks(sp, load_edges)

            sp.wait_ge(sums_added, CHUNKS)
            sp.dma_start(cnt_tiles[:, :], acc[0:1, 1, 0:N].rearrange("o (t p) -> o t p", p=NR)).then_inc(cnt_moved, 16)

            def store_out(g, b, n):
                sp.wait_ge(out_ready, g + 1)
                sp.dma_start(out_v[:, bass.ds(g * GT, GT), :], o_t[b][:, :, :]).then_inc(out_written[b], 16)
            groups(sp, store_out)
            for b in range(2):
                sp.wait_ge(out_written[b], 16 * (GROUPS // 2))

        @block.gpsimd
        def _(pool):
            nc.gpsimd.memset(ident[:, :], 0.0).then_inc(ident_clear, 1)
            pool.wait_ge(ident_clear, 1)
            nc.gpsimd.affine_select(out=ident[:, :], in_=ident[:, :], compare_op=ALU.not_equal, fill=1.0,
                                    base=0, pattern=[[-1, P]], channel_multiplier=1).then_inc(ident_ready, 1)
            nc.gpsimd.memset(eps[:, 0:1], EPS_X).then_inc(const_ready, 1)
            nc.gpsimd.memset(eps[:, 1:2], EPS_MLP).then_inc(const_ready, 1)
            nc.gpsimd.memset(ones[:, :], 1.0).then_inc(const_ready, 1)
            nc.gpsimd.memset(ones_bf[:, :], 1.0).then_inc(const_ready, 1)
            nc.gpsimd.iota(ramp_i[:, :], pattern=[[1, W]], base=0, channel_multiplier=0).then_inc(ramp_made, 1)
            pool.dma_start(cen[:, CEN_N2, :], Wn1[D:D + H, :]).then_inc(low_loaded, 16)
            for q in range(PACK):
                pool.dma_start(cen[q * DE:(q + 1) * DE, CEN_EDGE, :], We1[D:D + DE, :]).then_inc(low_loaded, 16)
            nc.gpsimd.memset(wedge[:, :, :], 0.0).then_inc(wedge_clear, 1)
            nc.gpsimd.memset(acc[:, :, :], 0.0).then_inc(sums_cleared, 1)

            def add_bias(g):
                pool.wait_ge(own_kept, g + 1)
                own = nodes[:, bass.ds(g * GT, GT), H:2 * H]
                nc.gpsimd.tensor_tensor(own, own, cen[0:NR, CEN_BN1, :].unsqueeze(1).to_broadcast([NR, GT, H]), ALU.add
                                        ).then_inc(own_ready, 1)

            def add_h(g, b, n):
                pool.wait_ge(h_ready, GT * (g + 1))
                xs = res[:, bass.ds(g * GT, GT), :].rearrange("p k f -> p (k f)")
                nc.gpsimd.tensor_tensor(xs, xs, h_t[b][:, :], ALU.add).then_inc(x_plus_h, 1)
                if at_least(g, 2):
                    add_bias(g - 2)
            groups(pool, add_h)
            add_bias(GROUPS - 2)
            add_bias(GROUPS - 1)

            for b in range(2):
                pool.wait_ge(table_written[b], 16 * (GROUPS // 2))

            def gather(c, b, n):
                r, s = size_of(c)
                if at_least(c, 2):
                    pool.wait_ge(z_ready, c - 1)
                pool.wait_ge(src_loaded[b], 16 * (n + 1))
                pool.sem_inc(gather_begun, 1)
                for j in range(s):
                    nc.gpsimd.indirect_dma_start(
                        out=rows[b][0:r, j, :], out_offset=None, in_=table[:, :],
                        in_offset=bass.IndirectOffsetOnAxis(ap=srcs[b][0:r, j:j + 1], axis=0),
                    ).then_inc(gathered[b], 16)
            chunks(pool, gather)

            def add_last_bias(g, b, n):
                xs = res[:, bass.ds(g * GT, GT), :]
                nc.gpsimd.tensor_tensor(xs, xs, vec[0:NR, V_BO, :].unsqueeze(1).to_broadcast([NR, GT, D]), ALU.add).then_inc(res_ready, 1)
            pool.wait_ge(late_loaded, 16 * 9)
            pool.wait_ge(x_plus_h, GROUPS)
            groups(pool, add_last_bias)

            def add_shift(g, b, n):
                if at_least(g, 1):
                    pool.wait_ge(own_full, g)
                nc.gpsimd.tensor_tensor(own_shift, shift[0:NR, :].unsqueeze(1).to_broadcast([NR, GT, H]),
                                        any_in[:, bass.ds(g * GT, GT)].unsqueeze(2).to_broadcast([NR, GT, H]), ALU.mult
                                        ).then_inc(shift_made, 1)
                pool.wait_ge(shift_made, g + 1)
                own = nodes[:, bass.ds(g * GT, GT), H:2 * H]
                nc.gpsimd.tensor_tensor(own, own, own_shift, ALU.add).then_inc(own_full, 1)
            pool.wait_ge(own_ready, GROUPS)
            pool.wait_ge(any_ready, 1)
            groups(pool, add_shift)

        @block.tensor
        def _(pe):
            pe.wait_ge(ident_ready, 1)

            def project_nodes(g, b):
                pe.wait_ge(hT_ready, g + 1)
                if at_least(g, 2):
                    pe.wait_ge(table_ready, g - 1)
                    pe.wait_ge(own_kept, g - 1)
                for t in range(GT):
                    last = nc.tensor.matmul(ps_nodes[b][0:NR, t * 2 * H:(t + 1) * 2 * H], hT[b][:, t * P:t * P + NR],
                                            cen[:, CEN_E1:CEN_N1 + 1, :], start=True, stop=True)
                last.then_inc(projected, 1)

            def node_step(g, b, n):
                if at_least(g, 1):
                    if isinstance(g, int) and g == 1:
                        pe.wait_ge(cen_ready, 1)
                    project_nodes(g - 1, 1 - b)
                pe.wait_ge(h_ready, GT * (g + 1))
                for t in range(GT):
                    last = nc.tensor.transpose(ps_hT[:, t * P:t * P + NR], h_t[b][:, t * D:(t + 1) * D], ident[0:NR, 0:NR])
                last.then_inc(h_transposed, 1)
            groups(pe, node_step)
            project_nodes(GROUPS - 1, 1)

            pe.wait_ge(late_loaded, 16 * 9)
            pe.wait_ge(table_ready, GROUPS - 1)
            pe.wait_ge(own_kept, GROUPS - 1)
            nc.tensor.transpose(banks(2, P), we2[:, :], ident[:, :]).then_inc(pe_prep, 1)
            nc.tensor.matmul(banks(3, 1), we2[:, :], cols[:, 0:1], start=True, stop=True).then_inc(pe_prep, 1)
            pe.wait_ge(prep, 2)
            pe.wait_ge(low_ready, 1)
            nc.tensor.matmul(banks(4, H), we2T[:, :], cen[:, CEN_N2, :], start=True, stop=True).then_inc(pe_prep, 1)
            nc.tensor.matmul(banks(0, H), shift_cols[:, :], cen[:, CEN_N2, :], start=True, stop=True).then_inc(pe_prep, 1)
            pe.wait_ge(prep, 4)
            pe.wait_ge(own_kept, GROUPS)
            nc.tensor.matmul(banks(5, 4 * HALF), ones[0:HALF, :], spread_diag[:, :, :, :].rearrange("p a b q -> p (a b q)"),
                             start=True, stop=True).then_inc(pe_prep, 1)
            pe.wait_ge(prep_ready, 1)

            windows = pe.alloc_register("pe_windows")
            pe.reg_mov(windows, 0)

            def window_sums(b, r, s, counter, counted, signal):
                for j in range(s):
                    nc.tensor.matmul(ps_sum[b][:, 0:W], msg[b][0:r, j, :], onehot[b][0:r, j, :], start=(j == 0), stop=(j == s - 1))
                for j in range(s):
                    last = nc.tensor.matmul(ps_sum[b][:, W:2 * W], counter[0:r, :], counted[b][0:r, j, :],
                                            start=(j == 0), stop=(j == s - 1))
                last.then_inc(signal, 1)

            def sum_messages(c, b):
                r, s = size_of(c)
                if at_least(c, 2):
                    pe.wait_ge(sums_added, c - 1)
                pe.wait_ge(onehot_bf_ready, c + 1)
                pe.wait_ge(message_ready, c + 1)
                window_sums(b, r, s, ones_bf, onehot_bf, sums_ready)
                more = pe.value_load(more_i[0:1, bass.ds(c, 1)], min_val=0, max_val=MOST)
                with pe.If(more > 0):
                    with pe.Fori(0, more):
                        pe.reg_add(windows, windows, 1)
                        pe.wait_ge(more_onehot, pe.snap(windows))
                        window_sums(b, r, s, ones, onehot, more_sums)

            def edge_step(c, b, n):
                r, s = size_of(c)
                pe.wait_ge(feat_loaded[b], 16 * (n + 1))
                if at_least(c, 2):
                    pe.wait_ge(featT_ready, c - 1)
                for q, k in packs_of(s):
                    last = nc.tensor.transpose(ps_featT[b][0:k * DE, q * P:q * P + r],
                                               feat[b][0:r, q * P:q * P + k * DE], ident[0:r, 0:r])
                last.then_inc(feat_transposed, 1)
                pe.wait_ge(featT_ready, c + 1)
                if at_least(c, 2):
                    pe.wait_ge(z_ready, c - 1)
                for q, k in packs_of(s):
                    last = nc.tensor.matmul(ps_edge[b][0:r, q * PACK * H:(q * PACK + k) * H],
                                            featT[b][0:k * DE, q * P:q * P + r],
                                            wedge[0:k * DE, 0:k, :], start=True, stop=True)
                last.then_inc(edge_projected, 1)
                if at_least(c, 2):
                    sum_messages(c - 2, b)
            chunks(pe, edge_step)
            for c in (CHUNKS - 2, CHUNKS - 1):
                sum_messages(c, c % 2)

            def aggregate(g, b):
                pe.wait_ge(staged, g + 1)
                for t in range(GT):
                    last = nc.tensor.matmul(ps_agg[b][0:NR, t * H:(t + 1) * H], agg[b][:, t * NR:(t + 1) * NR], fused[:, :],
                                            start=True, stop=True)
                last.then_inc(agg_projected, 1)

            aggregate(0, 0)
            pe.wait_ge(cnt_moved, 16)
            nc.tensor.transpose(ps_cnt, cnt_tiles[:, :], ident[0:TILES, 0:TILES]).then_inc(cnt_turned, 1)
            aggregate(1, 1)

            def last_step(g, b, n):
                pe.wait_ge(u_done, g + 1)
                if at_least(g, 1):
                    pe.wait_ge(uT_ready, g)
                for t in range(GT):
                    last = nc.tensor.transpose(ps_uT[:, t * P:t * P + NR], u[b][:, t, :], ident[0:NR, 0:NR])
                last.then_inc(u_transposed, 1)
                if not (isinstance(g, int) and g >= GROUPS - 2):
                    aggregate(g + 2, b)
                pe.wait_ge(uT_ready, g + 1)
                if at_least(g, 1):
                    pe.wait_ge(out_ready, g)
                for t in range(GT):
                    last = nc.tensor.matmul(ps_out[0:NR, t * D:(t + 1) * D], uT[b][:, t * P:t * P + NR], wn2[:, :],
                                            start=True, stop=True)
                last.then_inc(out_projected, 1)
            groups(pe, last_step)

        @block.scalar
        def _(act):
            def copy_hT(g, b):
                act.wait_ge(h_transposed, g + 1)
                if at_least(g, 2):
                    act.wait_ge(projected, g - 1)
                nc.scalar.copy(hT[b][:, :].rearrange("p (t c) -> p t c", c=P)[:, :, 0:NR],
                               ps_hT[:, :].rearrange("p (t c) -> p t c", c=P)[:, :, 0:NR]).then_inc(hT_ready, 1)

            def keep_own(g, b):
                act.wait_ge(table_ready, g + 1)
                nc.scalar.copy(nodes[:, bass.ds(g * GT, GT), H:2 * H],
                               ps_nodes[b][0:NR, 0:GT * 2 * H].rearrange("p (t c) -> p t c", t=GT)[:, :, H:2 * H]).then_inc(own_kept, 1)

            act.wait_ge(const_ready, 4)
            nc.scalar.activation(warm[:, :], eps[0:1, 0:1], ACT.Sqrt).then_inc(act_warm, 1)

            def node_step(g, b, n):
                act.wait_ge(aggr_done, g + 1)
                nc.scalar.activation(small[b][0:NR, S_STD, 0:GT], mv[b][:, :, 1], ACT.Sqrt, bias=eps[0:NR, 0:1]).then_inc(nstd_ready, 1)
                if at_least(g, 1):
                    copy_hT(g - 1, 1 - b)
                act.wait_ge(norm_ready, g + 1)
                if at_least(g, 2):
                    act.wait_ge(x_plus_h, g - 1)
                for t in range(GT):
                    nc.scalar.activation(h_t[b][:, t * D:(t + 1) * D], res[:, g * GT + t, :], ACT.Relu,
                                         bias=small[b][0:NR, S_NMR, t:t + 1], scale=small[b][0:NR, S_R, t:t + 1],
                                         ).then_inc(h_ready, 1)
                if at_least(g, 2):
                    keep_own(g - 2, b)
            groups(act, node_step)
            copy_hT(GROUPS - 1, 1)
            keep_own(GROUPS - 2, 0)
            keep_own(GROUPS - 1, 1)

            def cast_onehot(c, b):
                r, s = size_of(c)
                if at_least(c, 2):
                    act.wait_ge(sums_ready, c - 1)
                act.wait_ge(onehot_ready, c + 1)
                nc.scalar.copy(onehot_bf[b][0:r, 0:s, :], onehot[b][0:r, 0:s, :]).then_inc(onehot_bf_ready, 1)

            def edge_step(c, b, n):
                r, s = size_of(c)
                act.wait_ge(feat_transposed, c + 1)
                if at_least(c, 2):
                    act.wait_ge(edge_projected, c - 1)
                if r == P:
                    nc.scalar.copy(featT[b][:, :], ps_featT[b][:, :]).then_inc(featT_ready, 1)
                else:
                    for q, k in packs_of(s):
                        last = nc.scalar.copy(featT[b][0:k * DE, q * P:q * P + r], ps_featT[b][0:k * DE, q * P:q * P + r])
                    last.then_inc(featT_ready, 1)
                if at_least(c, 1):
                    cast_onehot(c - 1, 1 - b)
                act.wait_ge(z_ready, c + 1)
                if at_least(c, 2):
                    act.wait_ge(var_ready, c - 1)
                for j in range(s):
                    last = nc.scalar.activation(trash[0:r, j, :], z[b][0:r, j, :], ACT.Square, accum_out=squares[b][0:r, j:j + 1])
                last.then_inc(squares_done, 1)
                act.wait_ge(squares_done, c + 1)
                nc.scalar.activation(small[b][0:r, S_STD, 0:s], squares[b][0:r, 0:s], ACT.Sqrt,
                                     bias=eps[0:r, 1:2], scale=1.0 / H).then_inc(std_ready, 1)
            chunks(act, edge_step)
            cast_onehot(CHUNKS - 1, (CHUNKS - 1) % 2)

            def stage(g, b):
                if at_least(g, 2):
                    act.wait_ge(agg_projected, g - 1)
                nc.scalar.copy(agg[b], acc[:, 0, bass.ds(g * GT * NR, GT * NR)]).then_inc(staged, 1)

            act.wait_ge(sums_added, CHUNKS)
            stage(0, 0)
            stage(1, 1)

            def last_step(g, b, n):
                for t in range(GT):
                    act.wait_ge(u_ready, GT * g + t + 1)
                    last = nc.scalar.activation(trash[0:NR, t, :], u[b][:, t, :], ACT.Square, accum_out=squares[b][0:NR, t:t + 1])
                last.then_inc(u_squares, 1)
                act.wait_ge(u_squares, g + 1)
                nc.scalar.activation(small[b][0:NR, S_STD, 0:GT], squares[b][0:NR, 0:GT], ACT.Sqrt,
                                     bias=eps[0:NR, 1:2], scale=1.0 / H).then_inc(u_std, 1)
                if not (isinstance(g, int) and g >= GROUPS - 2):
                    stage(g + 2, b)
                act.wait_ge(u_transposed, g + 1)
                if at_least(g, 2):
                    act.wait_ge(out_projected, g - 1)
                nc.scalar.activation(uT[b][:, :].rearrange("p (t c) -> p t c", c=P)[:, :, 0:NR],
                                     ps_uT[:, :].rearrange("p (t c) -> p t c", c=P)[:, :, 0:NR], ACT.Relu,
                                     bias=cols[:, 3:4], scale=cols[:, 2:3]).then_inc(uT_ready, 1)
            groups(act, last_step)

        @block.vector
        def _(dve):
            def centre(first, count, step, ready):
                part, mean = cen[:, first:first + count, :], cen_mean[:, first:first + count]
                nc.vector.tensor_reduce(mean, part, AX.X, ALU.add).then_inc(step, 1)
                dve.wait_ge(step, 1)
                nc.vector.tensor_scalar(mean, mean, 1.0 / H, None, ALU.mult).then_inc(step, 1)
                dve.wait_ge(step, 2)
                nc.vector.tensor_tensor(part, part, mean.unsqueeze(2).to_broadcast([P, count, H]), ALU.subtract).then_inc(ready, 1)

            def keep_table(g, b):
                dve.wait_ge(projected, g + 1)
                nc.vector.tensor_tensor(nodes[:, bass.ds(g * GT, GT), 0:H],
                                        ps_nodes[b][0:NR, 0:GT * 2 * H].rearrange("p (t c) -> p t c", t=GT)[:, :, 0:H],
                                        cen[0:NR, CEN_BE1, :].unsqueeze(1).to_broadcast([NR, GT, H]), ALU.add).then_inc(table_ready, 1)

            def statistics(g, b, n):
                dve.wait_ge(x_loaded[b], 16 * (n + 1))
                for t in range(GT):
                    last = nc.vector.bn_stats(bn[b][:, t, :], res[:, g * GT + t, :])
                last.then_inc(bn_done, 1)
                if at_least(g, 2):
                    dve.wait_ge(norm_ready, g - 1)
                dve.wait_ge(bn_done, g + 1)
                dve.sem_inc(bn_seen, 1)
                for t in range(GT):
                    last = nc.vector.bn_aggr(mv[b][:, t, :], bn[b][:, t, :])
                last.then_inc(aggr_done, 1)

            def node_step(g, b, n):
                v, sd, r, a, q, nmr = (small[b][0:NR, k, 0:GT] for k in range(6))
                dve.wait_ge(aggr_done, g + 1)
                nc.vector.tensor_scalar(v, mv[b][:, :, 1], EPS_X, None, ALU.add).then_inc(nvar_ready, 1)
                if not (isinstance(g, int) and g == GROUPS - 1):
                    statistics(g + 1, 1 - b, n + b)
                dve.wait_ge(nvar_ready, g + 1)
                if at_least(g, 2):
                    dve.wait_ge(h_ready, GT * (g - 1))
                dve.wait_ge(nstd_ready, g + 1)
                inverse_root(dve, v, sd, r, a, q, nroot, 4 * g)
                nc.vector.scalar_tensor_tensor(nmr, mv[b][:, :, 0], -1.0, r, ALU.mult, ALU.mult).then_inc(norm_ready, 1)
                if isinstance(g, int) and g == 1:
                    dve.wait_ge(w_loaded, 16 * 4)
                    centre(CEN_E1, 4, cen_step, cen_ready)
                    dve.wait_ge(cen_ready, 1)
                if at_least(g, 2):
                    keep_table(g - 2, b)
            statistics(0, 0, 0)
            groups(dve, node_step)
            keep_table(GROUPS - 2, 0)
            keep_table(GROUPS - 1, 1)

            dve.wait_ge(low_loaded, 16 * (1 + PACK))
            centre(CEN_N2, 2, low_step, low_ready)
            dve.wait_ge(pe_prep, 1)
            nc.vector.tensor_copy(we2T[:, :], banks(2, P)).then_inc(prep, 1)
            dve.wait_ge(pe_prep, 2)
            nc.vector.tensor_tensor(shift_cols[:, :], banks(3, 1).to_broadcast([P, P]), cols[:, 1:2].to_broadcast([P, P]),
                                    ALU.add).then_inc(prep, 1)
            dve.wait_ge(ends_loaded, 16 * 3)
            for k, op in enumerate((ALU.min, ALU.max)):
                last = nc.vector.tensor_reduce(lohi[:, k, :], ends[:, :, :], AX.X, op)
            last.then_inc(prep, 1)
            dve.wait_ge(prep, 3)
            for k in range(2):
                for c in range(2):
                    last = nc.vector.tensor_scalar(spread_diag[:, k, c, :], ident[0:HALF, 0:HALF], lohi[:, k, c:c + 1], None, ALU.mult)
            last.then_inc(prep, 1)
            dve.wait_ge(low_ready, 1)
            dve.wait_ge(wedge_clear, 1)
            for q in range(PACK):
                nc.vector.tensor_copy(wedge[q * DE:(q + 1) * DE, q, :], cen[q * DE:(q + 1) * DE, CEN_EDGE, :]).then_inc(prep, 1)
            dve.wait_ge(late_loaded, 16 * 9)
            nc.vector.tensor_scalar(neg[:, :], vec[:, V_BE, :], -1.0, None, ALU.mult).then_inc(prep, 1)
            dve.wait_ge(ramp_made, 1)
            nc.vector.tensor_copy(ramp[:, :], ramp_i[:, :]).then_inc(prep, 1)
            dve.wait_ge(pe_prep, 3)
            nc.vector.tensor_copy(fused[:, :], banks(4, H)).then_inc(prep, 1)
            dve.wait_ge(pe_prep, 4)
            nc.vector.tensor_copy(shift[:, :], banks(0, H)).then_inc(prep, 1)
            dve.wait_ge(pe_prep, 5)
            bounds = banks(5, 4 * HALF).rearrange("p (k c q) -> p k q c", k=2, c=2)
            nc.vector.tensor_copy(base[:, :].rearrange("p (q c) -> p q c", c=2), bounds[:, 0, :, :]).then_inc(prep, 1)
            done = 4 + PACK + 5
            dve.wait_ge(prep, done)
            nc.vector.tensor_copy(base_i[:, :], base[0:1, :])
            nc.vector.tensor_tensor(reach[:, :].rearrange("p (q c) -> p q c", c=2), bounds[0:1, 1, :, :],
                                    base[0:1, :].rearrange("p (q c) -> p q c", c=2), ALU.subtract).then_inc(prep, 1)
            dve.wait_ge(prep, done + 1)
            nc.vector.tensor_copy(reach_i[:, :], reach[:, :]).then_inc(prep, 1)
            dve.wait_ge(prep, done + 2)
            nc.vector.tensor_scalar(more_i[:, :], reach_i[:, :], SHIFT, None, ALU.arith_shift_right).then_inc(prep_ready, 1)
            dve.wait_ge(prep_ready, 1)
            dve.wait_ge(sums_cleared, 1)

            windows = dve.alloc_register("dve_windows")
            dve.reg_mov(windows, 0)

            def make_onehot(b, r, s, signal):
                nc.vector.tensor_tensor(onehot[b][0:r, 0:s, :], ramp[0:r, :].unsqueeze(1).to_broadcast([r, s, W]),
                                        offs[b][0:r, 0:s].unsqueeze(2).to_broadcast([r, s, W]), ALU.is_equal).then_inc(signal, 1)

            def add_sums(c, b):
                r, s = size_of(c)
                dve.wait_ge(sums_ready, c + 1)
                if at_least(c, 1):
                    dve.wait_ge(sums_added, c)
                start = dve.value_load(base_i[0:1, bass.ds(c, 1)], min_val=0, max_val=N - 1)
                more = dve.value_load(more_i[0:1, bass.ds(c, 1)], min_val=0, max_val=MOST)
                window = acc[:, :, bass.ds(start, W)]
                sums = ps_sum[b][:, :].rearrange("p (k w) -> p k w", k=2)
                nc.vector.tensor_tensor(window, window, sums, ALU.add).then_inc(sums_added, 1)
                with dve.If(more > 0):
                    with dve.Fori(1, more + 1) as k:
                        dve.reg_add(windows, windows, 1)
                        w = dve.snap(windows)
                        dve.wait_ge(sums_added, c + 1)
                        nc.vector.tensor_scalar(offs[b][0:r, 0:s], offs[b][0:r, 0:s], -float(W), None, ALU.add).then_inc(more_offs, 1)
                        dve.wait_ge(more_offs, w)
                        make_onehot(b, r, s, more_onehot)
                        dve.wait_ge(more_sums, w)
                        far = nc.s_assert_within(start + k * W, 0, N - 1)
                        window = acc[:, :, bass.ds(far, W)]
                        nc.vector.tensor_tensor(window, window, sums, ALU.add).then_inc(more_added, 1)
                        dve.wait_ge(more_added, w)

            def normalise(c, b):
                r, s = size_of(c)
                v, sd, rs, a, q = (small[b][0:r, k, 0:s] for k in range(5))
                dve.wait_ge(squares_done, c + 1)
                nc.vector.tensor_scalar(v, squares[b][0:r, 0:s], 1.0 / H, EPS_MLP, ALU.mult, ALU.add).then_inc(var_ready, 1)
                dve.wait_ge(var_ready, c + 1)
                dve.wait_ge(std_ready, c + 1)
                inverse_root(dve, v, sd, rs, a, q, root, 4 * c)
                if at_least(c, 2):
                    dve.wait_ge(sums_ready, c - 1)
                for j in range(s):
                    last = nc.vector.scalar_tensor_tensor(msg[b][0:r, j, :], z[b][0:r, j, :], rs[:, j:j + 1], vec[0:r, V_GE, :],
                                                          ALU.mult, ALU.mult)
                last.then_inc(scaled, 1)
                dve.wait_ge(scaled, c + 1)
                nc.vector.tensor_tensor(msg[b][0:r, 0:s, :], msg[b][0:r, 0:s, :],
                                        neg[0:r, :].unsqueeze(1).to_broadcast([r, s, H]), ALU.max).then_inc(message_ready, 1)

            def edge_step(c, b, n):
                r, s = size_of(c)
                dve.wait_ge(edge_projected, c + 1)
                dve.wait_ge(gathered[b], 16 * SLOTS * n + 16 * s)
                nc.vector.tensor_tensor(z[b][0:r, 0:s, :], rows[b][0:r, 0:s, :],
                                        ps_edge[b][0:r, 0:s * H].rearrange("p (s h) -> p s h", s=s), ALU.add).then_inc(z_ready, 1)
                if at_least(c, 1):
                    normalise(c - 1, 1 - b)
                if at_least(c, 2):
                    add_sums(c - 2, b)
                dve.wait_ge(dst_loaded[b], 16 * (n + 1))
                nc.vector.tensor_scalar(offs[b][0:r, 0:s], dsts[b][0:r, 0:s], base[0:r, bass.ds(c, 1)], None, ALU.subtract
                                        ).then_inc(offs_ready, 1)
                dve.wait_ge(offs_ready, c + 1)
                make_onehot(b, r, s, onehot_ready)
            chunks(dve, edge_step)
            normalise(CHUNKS - 1, (CHUNKS - 1) % 2)
            for c in (CHUNKS - 2, CHUNKS - 1):
                add_sums(c, c % 2)

            dve.wait_ge(cnt_turned, 1)
            nc.vector.tensor_scalar(any_in[:, :], ps_cnt, 1.0, None, ALU.min).then_inc(any_ready, 1)
            nc.vector.tensor_scalar(recip[:, :], ps_cnt, 1.0, None, ALU.max).then_inc(cnt_one, 1)
            dve.wait_ge(cnt_one, 1)
            nc.vector.reciprocal(recip[:, :], recip[:, :]).then_inc(recip_ready, 1)
            dve.wait_ge(recip_ready, 1)

            def add_residual(g, b, n):
                dve.wait_ge(res_ready, g + 1)
                dve.wait_ge(out_projected, g + 1)
                if at_least(g, 2):
                    dve.wait_ge(out_written[b], 16 * n)
                nc.vector.tensor_tensor(o_t[b][:, :, :], ps_out[0:NR, :].rearrange("p (t c) -> p t c", t=GT),
                                        res[:, bass.ds(g * GT, GT), :], ALU.add).then_inc(out_ready, 1)

            def last_step(g, b, n):
                v, sd, rs, a, q = (small[b][0:NR, k, 0:GT] for k in range(5))
                dve.wait_ge(own_full, g + 1)
                dve.wait_ge(agg_projected, g + 1)
                if at_least(g, 2):
                    dve.wait_ge(u_transposed, g - 1)
                for t in range(GT):
                    nc.vector.scalar_tensor_tensor(u[b][:, t, :], ps_agg[b][0:NR, t * H:(t + 1) * H], recip[:, bass.ds(g * GT + t, 1)],
                                                   nodes[:, g * GT + t, H:2 * H], ALU.mult, ALU.add).then_inc(u_ready, 1)
                dve.wait_ge(u_squares, g + 1)
                nc.vector.tensor_scalar(v, squares[b][0:NR, 0:GT], 1.0 / H, EPS_MLP, ALU.mult, ALU.add).then_inc(u_var, 1)
                dve.wait_ge(u_var, g + 1)
                dve.wait_ge(u_std, g + 1)
                inverse_root(dve, v, sd, rs, a, q, u_root, 4 * g)
                nc.vector.tensor_tensor(u[b][:, :, :], u[b][:, :, :], rs.unsqueeze(2).to_broadcast([NR, GT, H]), ALU.mult).then_inc(u_done, 1)
                if at_least(g, 1):
                    add_residual(g - 1, 1 - b, n if b == 1 else n - 1)
            groups(dve, last_step)
            add_residual(GROUPS - 1, 1, GROUPS // 2 - 1)


_INS = ["x", "src", "dst", "edge_attr_32", "L0_gnn_We1", "L0_gnn_be1", "L0_gnn_ge1", "L0_gnn_ble1", "L0_gnn_We2", "L0_gnn_be2",
        "L0_gnn_Wn1", "L0_gnn_bn1", "L0_gnn_gn1", "L0_gnn_bln1", "L0_gnn_Wn2", "L0_gnn_bn2"]


def kernel(**inputs):
    import numpy as _np
    import concourse.bacc as _bacc
    from concourse import mybir as _mybir
    from concourse.bass_utils import run_bass_kernel_spmd as _run

    nc = _bacc.Bacc("TRN2", target_bir_lowering=False, num_devices=1)
    arrays, args = {}, []
    for name in _INS:
        a = _np.ascontiguousarray(inputs[name])
        arrays[f"in_{name}_dram"] = a
        args.append(nc.dram_tensor(f"in_{name}_dram", a.shape, _mybir.dt.from_np(a.dtype), kind="ExternalInput").ap())
    x = inputs["x"]
    args.append(nc.dram_tensor("out_0_dram", x.shape, _mybir.dt.from_np(_np.dtype(x.dtype)), kind="ExternalOutput").ap())
    graph_layer(nc, *args)
    r = _run(nc, [arrays], core_ids=[0])
    return r.results[0]["out_0_dram"]
```

```python
import concourse.bass as bass
from concourse import mybir
from contextlib import ExitStack


def graph_layer(nc, x, src, dst, edge, We1, be1, ge1, ble1, We2, be2, Wn1, bn1, gn1, bln1, Wn2, bn2, out):
    fp32 = mybir.dt.float32
    bf16 = mybir.dt.bfloat16
    i32 = mybir.dt.int32
    ALU = mybir.AluOpType
    ACT = mybir.ActivationFunctionType
    AX = mybir.AxisListType

    N, D = x.shape
    E, DE = edge.shape
    H = We2.shape[0]
    P = 128
    EPS_X = 1e-5
    EPS_MLP = 1e-6
    assert D == H == P

    SLOTS = 8
    CHUNK = P * SLOTS
    FULL = E // CHUNK
    TAIL = E - FULL * CHUNK
    TAIL_SLOTS = next(s for s in range(1, SLOTS + 1) if TAIL % s == 0 and TAIL // s <= P)
    TAIL_ROWS = TAIL // TAIL_SLOTS
    PAIRS = FULL // 2
    assert FULL % 2 == 1 and TAIL > 0
    CHUNKS = FULL + 1
    HALF = CHUNKS // 2
    W = 96
    MOST = (N - 1) // W
    assert W == 3 << 5 and all((x * 171) >> 9 == x // 3 for x in range((N >> 5) + 1))
    PACK = P // DE
    PACKS = SLOTS // PACK

    NR = 125
    TILES = N // NR
    GT = 5
    GROUPS = TILES // GT
    assert TILES * NR == N and GROUPS * GT == TILES and GROUPS % 2 == 0
    GW = GT * D
    CLEARS = 6
    CLEAR = -(-(N + W) // CLEARS)

    table = nc.dram_tensor("sender_table", (N, H), fp32).ap()
    x_v = x.rearrange("(k p) f -> p k f", p=NR)
    out_v = out.rearrange("(k p) f -> p k f", p=NR)
    table_v = table.rearrange("(k p) f -> p k f", p=NR)
    edge_v = edge[0:FULL * CHUNK, :].rearrange("(c p j) f -> c p (j f)", p=P, j=SLOTS)
    src_v = src[0:FULL * CHUNK].rearrange("(c p j) -> c p j", p=P, j=SLOTS)
    dst_v = dst[0:FULL * CHUNK].rearrange("(c p j) -> c p j", p=P, j=SLOTS)
    edge_t = edge[FULL * CHUNK:E, :].rearrange("(p j) f -> p (j f)", j=TAIL_SLOTS)
    src_t = src[FULL * CHUNK:E].rearrange("(p j) -> p j", j=TAIL_SLOTS)
    dst_t = dst[FULL * CHUNK:E].rearrange("(p j) -> p j", j=TAIL_SLOTS)

    ctx = ExitStack()
    with ctx:
        def sb(name, shape, dt=fp32):
            return ctx.enter_context(nc.sbuf_tensor(name, shape, dt))

        def sem(name):
            return ctx.enter_context(nc.semaphore(name))

        def two(name):
            return [sem(f"{name}{b}") for b in range(2)]

        acc = sb("acc", [P, 2, N + W])
        res = sb("res", [NR, TILES, D])
        nodes = sb("nodes", [NR, TILES, 2 * H])
        cen = sb("cen", [P, 6, H])
        CEN_E1, CEN_N1, CEN_BE1, CEN_BN1, CEN_N2, CEN_EDGE = range(6)
        cen_mean = sb("cen_mean", [P, 6])
        vec = sb("vec", [P, 3, H])
        V_GE, V_BE, V_BO = range(3)
        cols = sb("cols", [P, 4])
        we2 = sb("we2", [P, H])
        wn2 = sb("wn2", [P, D])
        we2T = sb("we2T", [P, H])
        fused = sb("fused", [P, H])
        shift_cols = sb("shift_cols", [P, P])
        shift = sb("shift", [P, H])
        eps = sb("eps", [P, 2])
        wedge = sb("wedge", [P, PACK, H])
        ident = sb("ident", [P, P])
        ones = sb("ones", [P, P])
        warm = sb("warm", [1, 1])
        ones_bf = sb("ones_bf", [P, P], bf16)
        ramp_i = sb("ramp_i", [P, W], i32)

        lohi = sb("lohi", [HALF, 2, 2])
        spread_diag = sb("spread_diag", [HALF, 2, 2, HALF])
        base = sb("base", [P, CHUNKS])
        base_i = sb("base_i", [1, CHUNKS], i32)
        reach = sb("reach", [1, CHUNKS])
        more_i = sb("more_i", [1, CHUNKS], i32)
        reach_i = sb("reach_i", [1, CHUNKS], i32)

        h_t = [sb(f"h_t{b}", [NR, GW]) for b in range(2)]
        hT = [sb(f"hT{b}", [P, GW]) for b in range(2)]
        bn = [sb(f"bn{b}", [NR, GT, 6]) for b in range(2)]
        mv = [sb(f"mv{b}", [NR, GT, 2]) for b in range(2)]
        small = [sb(f"small{b}", [P, 6, SLOTS]) for b in range(2)]
        S_VAR, S_STD, S_R, S_A, S_B, S_NMR = range(6)

        srcs = [sb(f"srcs{b}", [P, SLOTS], i32) for b in range(2)]
        dsts = [sb(f"dsts{b}", [P, SLOTS], i32) for b in range(2)]
        feat = [sb(f"feat{b}", [P, SLOTS * DE]) for b in range(2)]
        featT = [sb(f"featT{b}", [P, PACKS * P]) for b in range(2)]
        rows = [sb(f"rows{b}", [P, SLOTS, H]) for b in range(2)]
        z_two = sb("z_two", [P, 2, SLOTS, H])
        z = [z_two[:, b, :, :] for b in range(2)]
        ends = z_two[0:HALF, :, :, :].rearrange("q b s h -> q b (s h)").bitcast(i32)
        msg = [sb(f"msg{b}", [P, SLOTS, H]) for b in range(2)]
        offs = [sb(f"offs{b}", [P, SLOTS]) for b in range(2)]
        onehot = [sb(f"onehot{b}", [P, SLOTS, W]) for b in range(2)]
        onehot_bf = [sb(f"onehot_bf{b}", [P, SLOTS, W], bf16) for b in range(2)]
        squares = [sb(f"squares{b}", [P, SLOTS]) for b in range(2)]
        trash = sb("trash", [P, SLOTS, H], bf16)

        cnt_tiles = sb("cnt_tiles", [TILES, NR])
        recip = sb("recip", [NR, TILES])
        any_in = sb("any_in", [NR, TILES])
        agg = [rows[b][:, :, :].rearrange("p s h -> p (s h)")[:, 0:GT * NR] for b in range(2)]
        own_shift = onehot[0][0:NR, :, :].rearrange("p s w -> p (s w)")[:, 0:GT * H].rearrange("p (t h) -> p t h", t=GT)
        u = [z[b][0:NR, 0:GT, :] for b in range(2)]
        uT = hT
        o_t = [h_t[b][:, :].rearrange("p (t c) -> p t c", t=GT) for b in range(2)]

        ps = ctx.enter_context(nc.psum_tensor("ps", [P, 8, 512], fp32))
        flat = ps[:, :, :].rearrange("p b c -> p (b c)")

        def banks(first, width, rows=P):
            return flat[0:rows, 512 * first:512 * first + width]

        ps_hT = banks(0, GW)
        ps_nodes = [banks(2 + 3 * b, 3 * 512) for b in range(2)]
        ps_edge = [banks(2 * b, SLOTS * H) for b in range(2)]
        ps_featT = banks(4, PACKS * P)
        scale = banks(5, H)
        neg = banks(5, 2 * H)[:, H:]
        ramp = banks(5, 2 * H + W)[:, 2 * H:]
        ps_sum = [banks(6 + b, 2 * W) for b in range(2)]
        ps_agg = [banks(2 * b, 1024) for b in range(2)]
        ps_cnt = banks(0, 768 + TILES, NR)[:, 768:]
        ps_uT = banks(4, GW)
        ps_out = banks(6, GW)

        w_loaded = sem("w_loaded")
        low_loaded = sem("low_loaded")
        late_loaded = sem("late_loaded")
        ends_loaded = sem("ends_loaded")
        ident_clear, ident_ready, const_ready = sem("ident_clear"), sem("ident_ready"), sem("const_ready")
        ramp_made, sums_cleared, wedge_clear = sem("ramp_made"), sem("sums_cleared"), sem("wedge_clear")
        cen_step, cen_ready = sem("cen_step"), sem("cen_ready")
        low_step, low_ready = sem("low_step"), sem("low_ready")
        prep = sem("prep")
        pe_prep = sem("pe_prep")
        prep_ready = sem("prep_ready")
        x_loaded = two("x_loaded")
        bn_done, bn_seen, aggr_done = sem("bn_done"), sem("bn_seen"), sem("aggr_done")
        nvar_ready, nstd_ready = sem("nvar_ready"), sem("nstd_ready")
        nroot = sem("nroot")
        norm_ready = sem("norm_ready")
        h_ready, h_transposed, hT_ready = sem("h_ready"), sem("h_transposed"), sem("hT_ready")
        projected = sem("projected")
        table_ready, own_kept, own_ready = sem("table_ready"), sem("own_kept"), sem("own_ready")
        x_plus_h = sem("x_plus_h")
        table_written = two("table_written")
        feat_loaded, src_loaded, dst_loaded = two("feat_loaded"), two("src_loaded"), two("dst_loaded")
        gathered = two("gathered")
        gather_begun = sem("gather_begun")
        feat_transposed, featT_ready, edge_projected = sem("feat_transposed"), sem("featT_ready"), sem("edge_projected")
        offs_ready, onehot_ready, onehot_bf_ready = sem("offs_ready"), sem("onehot_ready"), sem("onehot_bf_ready")
        z_ready, squares_done, var_ready, std_ready = sem("z_ready"), sem("squares_done"), sem("var_ready"), sem("std_ready")
        root = sem("root")
        scaled, message_ready = sem("scaled"), sem("message_ready")
        sums_ready, sums_added, totals_ready = sem("sums_ready"), sem("sums_added"), sem("totals_ready")
        more_offs, more_onehot, more_sums, more_added = sem("more_offs"), sem("more_onehot"), sem("more_sums"), sem("more_added")
        cnt_moved, cnt_turned, cnt_one, recip_ready = sem("cnt_moved"), sem("cnt_turned"), sem("cnt_one"), sem("recip_ready")
        any_ready, shift_made, own_full = sem("any_ready"), sem("shift_made"), sem("own_full")
        first_own = sem("first_own")
        act_warm = sem("act_warm")
        res_ready, staged, agg_projected = sem("res_ready"), sem("staged"), sem("agg_projected")
        u_ready, u_squares, u_var, u_std = sem("u_ready"), sem("u_squares"), sem("u_var"), sem("u_std")
        u_root = sem("u_root")
        u_done, u_transposed, uT_ready = sem("u_done"), sem("u_transposed"), sem("uT_ready")
        out_projected, out_ready = sem("out_projected"), sem("out_ready")
        out_written = two("out_written")

        def in_pairs(eng, body, steps, first, last):
            for s in range(2 * first):
                body(s, s % 2, s // 2)
            with eng.Fori(first, last) as i:
                for b in range(2):
                    body(2 * i + b, b, i)
            for s in range(2 * last, steps):
                body(s, s % 2, s // 2)

        def chunks(eng, body):
            in_pairs(eng, body, CHUNKS, 2, PAIRS)

        def groups(eng, body):
            in_pairs(eng, body, GROUPS, 2, GROUPS // 2 - 1)

        def last_groups(body):
            for g in range(GROUPS):
                body(g, g % 2, g // 2)

        def at_least(step, k):
            return (step if isinstance(step, int) else step.min_val) >= k

        def size_of(c):
            tail = isinstance(c, int) and c == CHUNKS - 1
            return (TAIL_ROWS, TAIL_SLOTS) if tail else (P, SLOTS)

        def packs_of(slots):
            return [(q, min(PACK, slots - q * PACK)) for q in range((slots + PACK - 1) // PACK)]

        def inverse_root(dve, var, std, r, a, b, done, at):
            nc.vector.reciprocal(r, std).then_inc(done, 1)
            dve.wait_ge(done, at + 1)
            nc.vector.scalar_tensor_tensor(a, var, -0.5, r, ALU.mult, ALU.mult).then_inc(done, 1)
            dve.wait_ge(done, at + 2)
            nc.vector.tensor_tensor(b, a, r, ALU.mult).then_inc(done, 1)
            dve.wait_ge(done, at + 3)
            nc.vector.scalar_tensor_tensor(r, b, 1.5, r, ALU.add, ALU.mult).then_inc(done, 1)
            dve.wait_ge(done, at + 4)

        def spread(v):
            return v.unsqueeze(0).to_broadcast([P, H])

        block = ctx.enter_context(nc.Block())

        @block.sync
        def _(sp):
            def load_x(g, b, n):
                if at_least(g, 2):
                    sp.wait_ge(x_loaded[b], 16 * n)
                sp.dma_start(res[:, bass.ds(g * GT, GT), :], x_v[:, bass.ds(g * GT, GT), :]).then_inc(x_loaded[b], 16)
                if isinstance(g, int) and g == 1:
                    for slot, w in ((CEN_E1, We1[0:D, :]), (CEN_N1, Wn1[0:D, :]), (CEN_BE1, spread(be1)), (CEN_BN1, spread(bn1))):
                        sp.dma_start(cen[:, slot, :], w).then_inc(w_loaded, 16)
            groups(sp, load_x)

            sp.dma_start(ends[0:HALF - 1, :, :], dst[0:(HALF - 1) * 2 * CHUNK].rearrange("(q c e) -> q c e", c=2, e=CHUNK)
                         ).then_inc(ends_loaded, 16)
            sp.dma_start(ends[HALF - 1:HALF, 0, :], dst[(FULL - 1) * CHUNK:FULL * CHUNK].unsqueeze(0)).then_inc(ends_loaded, 16)
            sp.dma_start(ends[HALF - 1:HALF, 1, :], dst[E - CHUNK:E].unsqueeze(0)).then_inc(ends_loaded, 16)
            for slot, w in ((V_GE, ge1), (V_BE, ble1), (V_BO, bn2)):
                sp.dma_start(vec[:, slot, :], spread(w)).then_inc(late_loaded, 16)
            sp.dma_start(we2[:, :], We2).then_inc(late_loaded, 16)
            sp.dma_start(wn2[:, :], Wn2).then_inc(late_loaded, 16)
            for k, v in enumerate((ble1, be2, gn1, bln1)):
                sp.dma_start(cols[:, k:k + 1], v.unsqueeze(1)).then_inc(late_loaded, 16)

            for g in range(GROUPS):
                if g >= 2:
                    sp.wait_ge(table_written[g % 2], 16 * (g // 2))
                sp.wait_ge(table_ready, g + 1)
                sp.dma_start(table_v[:, g * GT:(g + 1) * GT, :], nodes[:, g * GT:(g + 1) * GT, 0:H]).then_inc(table_written[g % 2], 16)

            def load_edges(c, b, n):
                r, s = size_of(c)
                if r == P:
                    fs, ss, ds = edge_v[c, :, :], src_v[c, :, :], dst_v[c, :, :]
                else:
                    fs, ss, ds = edge_t, src_t, dst_t
                if at_least(c, 2):
                    sp.wait_ge(feat_transposed, c - 1)
                sp.dma_start(feat[b][0:r, 0:s * DE], fs).then_inc(feat_loaded[b], 16)
                if at_least(c, 2):
                    sp.wait_ge(gathered[b], 16 * SLOTS * n)
                sp.dma_start(srcs[b][0:r, 0:s], ss).then_inc(src_loaded[b], 16)
                if at_least(c, 2):
                    sp.wait_ge(offs_ready, c - 1)
                sp.dma_start(dsts[b][0:r, 0:s], ds).then_inc(dst_loaded[b], 16)
            chunks(sp, load_edges)

            sp.wait_ge(totals_ready, 1)
            sp.dma_start(cnt_tiles[:, :], acc[0:1, 1, 0:N].rearrange("o (t p) -> o t p", p=NR)).then_inc(cnt_moved, 16)

            def store_out(g, b, n):
                sp.wait_ge(out_ready, g + 1)
                sp.dma_start(out_v[:, bass.ds(g * GT, GT), :], o_t[b][:, :, :]).then_inc(out_written[b], 16)
            last_groups(store_out)
            for b in range(2):
                sp.wait_ge(out_written[b], 16 * (GROUPS // 2))

        @block.gpsimd
        def _(pool):
            nc.gpsimd.memset(ident[:, :], 0.0).then_inc(ident_clear, 1)
            pool.wait_ge(ident_clear, 1)
            nc.gpsimd.affine_select(out=ident[:, :], in_=ident[:, :], compare_op=ALU.not_equal, fill=1.0,
                                    base=0, pattern=[[-1, P]], channel_multiplier=1).then_inc(ident_ready, 1)
            nc.gpsimd.memset(eps[:, 0:1], EPS_X).then_inc(const_ready, 1)
            nc.gpsimd.memset(eps[:, 1:2], EPS_MLP).then_inc(const_ready, 1)
            nc.gpsimd.memset(ones[:, :], 1.0).then_inc(const_ready, 1)
            nc.gpsimd.memset(ones_bf[:, :], 1.0).then_inc(const_ready, 1)
            nc.gpsimd.iota(ramp_i[:, :], pattern=[[1, W]], base=0, channel_multiplier=0).then_inc(ramp_made, 1)
            pool.dma_start(cen[:, CEN_N2, :], Wn1[D:D + H, :]).then_inc(low_loaded, 16)
            for q in range(PACK):
                pool.dma_start(cen[q * DE:(q + 1) * DE, CEN_EDGE, :], We1[D:D + DE, :]).then_inc(low_loaded, 16)
            nc.gpsimd.memset(wedge[:, :, :], 0.0).then_inc(wedge_clear, 1)
            nc.gpsimd.memset(acc[:, 1, :], 0.0).then_inc(sums_cleared, 1)

            def add_bias(g):
                pool.wait_ge(own_kept, g + 1)
                own = nodes[:, bass.ds(g * GT, GT), H:2 * H]
                nc.gpsimd.tensor_tensor(own, own, cen[0:NR, CEN_BN1, :].unsqueeze(1).to_broadcast([NR, GT, H]), ALU.add
                                        ).then_inc(own_ready, 1)

            def add_h(g, b, n):
                pool.wait_ge(h_ready, GT * (g + 1))
                xs = res[:, bass.ds(g * GT, GT), :].rearrange("p k f -> p (k f)")
                nc.gpsimd.tensor_tensor(xs, xs, h_t[b][:, :], ALU.add).then_inc(x_plus_h, 1)
                if isinstance(g, int):
                    part = g if g < 4 else g - (GROUPS - CLEARS)
                    nc.gpsimd.memset(acc[:, 0, part * CLEAR:min(N + W, (part + 1) * CLEAR)], 0.0).then_inc(sums_cleared, 1)
                if at_least(g, 2):
                    add_bias(g - 2)
            groups(pool, add_h)
            add_bias(GROUPS - 2)

            for b in range(2):
                pool.wait_ge(table_written[b], 16 * (GROUPS // 2))

            def gather(c, b, n):
                r, s = size_of(c)
                if at_least(c, 2):
                    pool.wait_ge(z_ready, c - 1)
                pool.wait_ge(src_loaded[b], 16 * (n + 1))
                pool.sem_inc(gather_begun, 1)
                for j in range(s):
                    nc.gpsimd.indirect_dma_start(
                        out=rows[b][0:r, j, :], out_offset=None, in_=table[:, :],
                        in_offset=bass.IndirectOffsetOnAxis(ap=srcs[b][0:r, j:j + 1], axis=0),
                    ).then_inc(gathered[b], 16)
            chunks(pool, gather)

            def add_last_bias(g, b, n):
                xs = res[:, bass.ds(g * GT, GT), :]
                nc.gpsimd.tensor_tensor(xs, xs, vec[0:NR, V_BO, :].unsqueeze(1).to_broadcast([NR, GT, D]), ALU.add).then_inc(res_ready, 1)
            add_bias(GROUPS - 1)
            pool.wait_ge(late_loaded, 16 * 9)
            pool.wait_ge(x_plus_h, GROUPS)
            groups(pool, add_last_bias)

            pool.wait_ge(own_ready, GROUPS)
            pool.wait_ge(any_ready, 1)
            def add_shift(g):
                if at_least(g, 2):
                    pool.wait_ge(own_full, g - 1)
                nc.gpsimd.tensor_tensor(own_shift, shift[0:NR, :].unsqueeze(1).to_broadcast([NR, GT, H]),
                                        any_in[:, bass.ds(g * GT, GT)].unsqueeze(2).to_broadcast([NR, GT, H]), ALU.mult
                                        ).then_inc(shift_made, 1)
                pool.wait_ge(shift_made, g)
                own = nodes[:, bass.ds(g * GT, GT), H:2 * H]
                nc.gpsimd.tensor_tensor(own, own, own_shift, ALU.add).then_inc(own_full, 1)
            add_shift(1)
            with pool.Fori(2, GROUPS) as g:
                add_shift(g)

        @block.tensor
        def _(pe):
            pe.wait_ge(ident_ready, 1)

            def keep_clock_up(count, at):
                for _ in range(count):
                    nc.tensor.matmul(at, ident[:, :], ident[:, :], start=True, stop=True)

            keep_clock_up(24, banks(7, P))

            def project_nodes(g, b):
                pe.wait_ge(hT_ready, g + 1)
                if at_least(g, 2):
                    pe.wait_ge(table_ready, g - 1)
                    pe.wait_ge(own_kept, g - 1)
                for t in range(GT):
                    last = nc.tensor.matmul(ps_nodes[b][0:NR, t * 2 * H:(t + 1) * 2 * H], hT[b][:, t * P:t * P + NR],
                                            cen[:, CEN_E1:CEN_N1 + 1, :], start=True, stop=True)
                last.then_inc(projected, 1)

            def node_step(g, b, n):
                if at_least(g, 1):
                    if isinstance(g, int) and g == 1:
                        pe.wait_ge(cen_ready, 1)
                    project_nodes(g - 1, 1 - b)
                pe.wait_ge(h_ready, GT * (g + 1))
                for t in range(GT):
                    last = nc.tensor.transpose(ps_hT[:, t * P:t * P + NR], h_t[b][:, t * D:(t + 1) * D], ident[0:NR, 0:NR])
                last.then_inc(h_transposed, 1)
            groups(pe, node_step)
            project_nodes(GROUPS - 1, 1)

            pe.wait_ge(late_loaded, 16 * 9)
            pe.wait_ge(table_ready, GROUPS - 1)
            pe.wait_ge(own_kept, GROUPS - 1)
            nc.tensor.transpose(banks(2, P), we2[:, :], ident[:, :]).then_inc(pe_prep, 1)
            nc.tensor.matmul(banks(3, 1), we2[:, :], cols[:, 0:1], start=True, stop=True).then_inc(pe_prep, 1)
            pe.wait_ge(prep, 2)
            pe.wait_ge(low_ready, 1)
            nc.tensor.matmul(banks(4, H), we2T[:, :], cen[:, CEN_N2, :], start=True, stop=True).then_inc(pe_prep, 1)
            nc.tensor.matmul(banks(0, H), shift_cols[:, :], cen[:, CEN_N2, :], start=True, stop=True).then_inc(pe_prep, 1)
            pe.wait_ge(prep, 4)
            pe.wait_ge(own_kept, GROUPS)
            nc.tensor.matmul(banks(6, 4 * HALF), ones[0:HALF, :], spread_diag[:, :, :, :].rearrange("p a b q -> p (a b q)"),
                             start=True, stop=True).then_inc(pe_prep, 1)
            pe.wait_ge(prep_ready, 1)

            windows = pe.alloc_register("pe_windows")
            pe.reg_mov(windows, 0)

            def count_window(b, r, s, counter, counted):
                for j in range(s):
                    nc.tensor.matmul(ps_sum[b][:, W:2 * W], counter[0:r, :], counted[b][0:r, j, :], start=(j == 0), stop=(j == s - 1))

            def sum_window(b, r, s, signal):
                for j in range(s):
                    last = nc.tensor.matmul(ps_sum[b][:, 0:W], msg[b][0:r, j, :], onehot[b][0:r, j, :],
                                            start=(j == 0), stop=(j == s - 1))
                last.then_inc(signal, 1)

            def sum_messages(c, b):
                r, s = size_of(c)
                if at_least(c, 2):
                    pe.wait_ge(sums_added, c - 1)
                pe.wait_ge(onehot_bf_ready, c + 1)
                count_window(b, r, s, ones_bf, onehot_bf)
                pe.wait_ge(message_ready, 2 * (c + 1))
                sum_window(b, r, s, sums_ready)
                more = pe.value_load(more_i[0:1, bass.ds(c, 1)], min_val=0, max_val=MOST)
                with pe.If(more > 0):
                    with pe.Fori(0, more):
                        pe.reg_add(windows, windows, 1)
                        pe.wait_ge(more_onehot, pe.snap(windows))
                        count_window(b, r, s, ones, onehot)
                        sum_window(b, r, s, more_sums)

            def edge_step(c, b, n):
                r, s = size_of(c)
                pe.wait_ge(feat_loaded[b], 16 * (n + 1))
                for q, k in packs_of(s):
                    last = nc.tensor.transpose(ps_featT[0:k * DE, q * P:q * P + r],
                                               feat[b][0:r, q * P:q * P + k * DE], ident[0:r, 0:r])
                last.then_inc(feat_transposed, 1)
                pe.wait_ge(featT_ready, c + 1)
                if at_least(c, 2):
                    pe.wait_ge(z_ready, c - 1)
                for q, k in packs_of(s):
                    last = nc.tensor.matmul(ps_edge[b][0:r, q * PACK * H:(q * PACK + k) * H],
                                            featT[b][0:k * DE, q * P:q * P + r],
                                            wedge[0:k * DE, 0:k, :], start=True, stop=True)
                last.then_inc(edge_projected, 1)
                if at_least(c, 2):
                    sum_messages(c - 2, b)
            chunks(pe, edge_step)
            for c in (CHUNKS - 2, CHUNKS - 1):
                keep_clock_up(12, ps_featT[:, 0:P])
                sum_messages(c, c % 2)

            def aggregate(g, b):
                pe.wait_ge(staged, g + 1)
                for t in range(GT):
                    last = nc.tensor.matmul(ps_agg[b][0:NR, t * H:(t + 1) * H], agg[b][:, t * NR:(t + 1) * NR], fused[:, :],
                                            start=True, stop=True)
                last.then_inc(agg_projected, 1)

            keep_clock_up(6, banks(4, P))
            aggregate(0, 0)
            pe.wait_ge(cnt_moved, 16)
            nc.tensor.transpose(ps_cnt, cnt_tiles[:, :], ident[0:TILES, 0:TILES]).then_inc(cnt_turned, 1)
            aggregate(1, 1)
            keep_clock_up(20, banks(4, P))
            pe.wait_ge(u_ready, GT)
            aggregate(2, 0)

            def last_step(g, b, n):
                pe.wait_ge(u_done, g + 1)
                if at_least(g, 1):
                    pe.wait_ge(uT_ready, g)
                for t in range(GT):
                    last = nc.tensor.transpose(ps_uT[:, t * P:t * P + NR], u[b][:, t, :], ident[0:NR, 0:NR])
                last.then_inc(u_transposed, 1)
                if g < GROUPS - 3:
                    aggregate(g + 3, 1 - b)
                if at_least(g, 1):
                    pe.wait_ge(out_ready, g)
                pe.wait_ge(uT_ready, g + 1)
                for t in range(GT):
                    last = nc.tensor.matmul(ps_out[0:NR, t * D:(t + 1) * D], uT[b][:, t * P:t * P + NR], wn2[:, :],
                                            start=True, stop=True)
                last.then_inc(out_projected, 1)
            last_groups(last_step)

        @block.scalar
        def _(act):
            def copy_hT(g, b):
                act.wait_ge(h_transposed, g + 1)
                if at_least(g, 2):
                    act.wait_ge(projected, g - 1)
                nc.scalar.copy(hT[b][:, :].rearrange("p (t c) -> p t c", c=P)[:, :, 0:NR],
                               ps_hT[:, :].rearrange("p (t c) -> p t c", c=P)[:, :, 0:NR]).then_inc(hT_ready, 1)

            def keep_own(g, b):
                act.wait_ge(table_ready, g + 1)
                nc.scalar.copy(nodes[:, bass.ds(g * GT, GT), H:2 * H],
                               ps_nodes[b][0:NR, 0:GT * 2 * H].rearrange("p (t c) -> p t c", t=GT)[:, :, H:2 * H]).then_inc(own_kept, 1)

            act.wait_ge(const_ready, 4)
            nc.scalar.activation(warm[:, :], eps[0:1, 0:1], ACT.Sqrt).then_inc(act_warm, 1)

            def node_deviation(g, b):
                act.wait_ge(aggr_done, g + 1)
                nc.scalar.activation(small[b][0:NR, S_STD, 0:GT], mv[b][:, :, 1], ACT.Sqrt, bias=eps[0:NR, 0:1]).then_inc(nstd_ready, 1)

            def node_step(g, b, n):
                if at_least(g, 1):
                    copy_hT(g - 1, 1 - b)
                if not (isinstance(g, int) and g == GROUPS - 1):
                    node_deviation(g + 1, 1 - b)
                act.wait_ge(norm_ready, g + 1)
                if at_least(g, 2):
                    act.wait_ge(x_plus_h, g - 1)
                for t in range(GT):
                    nc.scalar.activation(h_t[b][:, t * D:(t + 1) * D], res[:, g * GT + t, :], ACT.Relu,
                                         bias=small[b][0:NR, S_NMR, t:t + 1], scale=small[b][0:NR, S_R, t:t + 1],
                                         ).then_inc(h_ready, 1)
                if at_least(g, 2):
                    keep_own(g - 2, b)
            node_deviation(0, 0)
            groups(act, node_step)
            copy_hT(GROUPS - 1, 1)
            keep_own(GROUPS - 2, 0)
            keep_own(GROUPS - 1, 1)

            def cast_onehot(c, b):
                r, s = size_of(c)
                if at_least(c, 2):
                    act.wait_ge(sums_ready, c - 1)
                act.wait_ge(onehot_ready, c + 1)
                nc.scalar.copy(onehot_bf[b][0:r, 0:s, :], onehot[b][0:r, 0:s, :]).then_inc(onehot_bf_ready, 1)

            def edge_step(c, b, n):
                r, s = size_of(c)
                act.wait_ge(feat_transposed, c + 1)
                if at_least(c, 2):
                    act.wait_ge(edge_projected, c - 1)
                if r == P:
                    nc.scalar.copy(featT[b][:, :], ps_featT[:, :]).then_inc(featT_ready, 1)
                else:
                    for q, k in packs_of(s):
                        last = nc.scalar.copy(featT[b][0:k * DE, q * P:q * P + r], ps_featT[0:k * DE, q * P:q * P + r])
                    last.then_inc(featT_ready, 1)
                if at_least(c, 1):
                    cast_onehot(c - 1, 1 - b)
                act.wait_ge(z_ready, c + 1)
                for j in range(s):
                    last = nc.scalar.activation(trash[0:r, j, :], z[b][0:r, j, :], ACT.Square, accum_out=squares[b][0:r, j:j + 1])
                last.then_inc(squares_done, 1)
                act.wait_ge(squares_done, c + 1)
                nc.scalar.activation(small[b][0:r, S_STD, 0:s], squares[b][0:r, 0:s], ACT.Sqrt,
                                     bias=eps[0:r, 1:2], scale=1.0 / H).then_inc(std_ready, 1)
                nc.scalar.activation(small[b][0:r, S_VAR, 0:s], squares[b][0:r, 0:s], ACT.Identity,
                                     bias=eps[0:r, 1:2], scale=1.0 / H).then_inc(var_ready, 1)
            chunks(act, edge_step)
            cast_onehot(CHUNKS - 1, (CHUNKS - 1) % 2)

            def stage(g, b):
                if at_least(g, 2):
                    act.wait_ge(agg_projected, g - 1)
                nc.scalar.copy(agg[b], acc[:, 0, bass.ds(g * GT * NR, GT * NR)]).then_inc(staged, 1)

            act.wait_ge(totals_ready, 1)
            stage(0, 0)
            stage(1, 1)

            def deviation(g, b):
                for t in range(GT):
                    act.wait_ge(u_ready, GT * g + t + 1)
                    last = nc.scalar.activation(trash[0:NR, t, :], u[b][:, t, :], ACT.Square, accum_out=squares[b][0:NR, t:t + 1])
                last.then_inc(u_squares, 1)
                act.wait_ge(u_squares, g + 1)
                nc.scalar.activation(small[b][0:NR, S_STD, 0:GT], squares[b][0:NR, 0:GT], ACT.Sqrt,
                                     bias=eps[0:NR, 1:2], scale=1.0 / H).then_inc(u_std, 1)
                nc.scalar.activation(small[b][0:NR, S_VAR, 0:GT], squares[b][0:NR, 0:GT], ACT.Identity,
                                     bias=eps[0:NR, 1:2], scale=1.0 / H).then_inc(u_var, 1)

            def last_step(g, b, n):
                if g < GROUPS - 1:
                    deviation(g + 1, 1 - b)
                if g < GROUPS - 3:
                    stage(g + 3, 1 - b)
                act.wait_ge(u_transposed, g + 1)
                if at_least(g, 2):
                    act.wait_ge(out_projected, g - 1)
                nc.scalar.activation(uT[b][:, :].rearrange("p (t c) -> p t c", c=P)[:, :, 0:NR],
                                     ps_uT[:, :].rearrange("p (t c) -> p t c", c=P)[:, :, 0:NR], ACT.Relu,
                                     bias=cols[:, 3:4], scale=cols[:, 2:3]).then_inc(uT_ready, 1)
            deviation(0, 0)
            stage(2, 0)
            last_groups(last_step)

        @block.vector
        def _(dve):
            def centre(first, count, step, ready):
                part, mean = cen[:, first:first + count, :], cen_mean[:, first:first + count]
                nc.vector.tensor_reduce(mean, part, AX.X, ALU.add).then_inc(step, 1)
                dve.wait_ge(step, 1)
                nc.vector.tensor_scalar(mean, mean, 1.0 / H, None, ALU.mult).then_inc(step, 1)
                dve.wait_ge(step, 2)
                nc.vector.tensor_tensor(part, part, mean.unsqueeze(2).to_broadcast([P, count, H]), ALU.subtract).then_inc(ready, 1)

            def keep_table(g, b):
                dve.wait_ge(projected, g + 1)
                nc.vector.tensor_tensor(nodes[:, bass.ds(g * GT, GT), 0:H],
                                        ps_nodes[b][0:NR, 0:GT * 2 * H].rearrange("p (t c) -> p t c", t=GT)[:, :, 0:H],
                                        cen[0:NR, CEN_BE1, :].unsqueeze(1).to_broadcast([NR, GT, H]), ALU.add).then_inc(table_ready, 1)

            def statistics(g, b, n):
                dve.wait_ge(x_loaded[b], 16 * (n + 1))
                for t in range(GT):
                    last = nc.vector.bn_stats(bn[b][:, t, :], res[:, g * GT + t, :])
                last.then_inc(bn_done, 1)
                if at_least(g, 2):
                    dve.wait_ge(norm_ready, g - 1)
                dve.wait_ge(bn_done, g + 1)
                dve.sem_inc(bn_seen, 1)
                for t in range(GT):
                    last = nc.vector.bn_aggr(mv[b][:, t, :], bn[b][:, t, :])
                last.then_inc(aggr_done, 1)

            def node_step(g, b, n):
                v, sd, r, a, q, nmr = (small[b][0:NR, k, 0:GT] for k in range(6))
                dve.wait_ge(aggr_done, g + 1)
                nc.vector.tensor_scalar(v, mv[b][:, :, 1], EPS_X, None, ALU.add).then_inc(nvar_ready, 1)
                if not (isinstance(g, int) and g == GROUPS - 1):
                    statistics(g + 1, 1 - b, n + b)
                dve.wait_ge(nvar_ready, g + 1)
                if at_least(g, 2):
                    dve.wait_ge(h_ready, GT * (g - 1))
                dve.wait_ge(nstd_ready, g + 1)
                inverse_root(dve, v, sd, r, a, q, nroot, 4 * g)
                nc.vector.scalar_tensor_tensor(nmr, mv[b][:, :, 0], -1.0, r, ALU.mult, ALU.mult).then_inc(norm_ready, 1)
                if isinstance(g, int) and g == 0:
                    dve.wait_ge(w_loaded, 16 * 4)
                    centre(CEN_E1, 4, cen_step, cen_ready)
                    dve.wait_ge(cen_ready, 1)
                if at_least(g, 2):
                    keep_table(g - 2, b)
            statistics(0, 0, 0)
            groups(dve, node_step)
            keep_table(GROUPS - 2, 0)
            keep_table(GROUPS - 1, 1)

            dve.wait_ge(low_loaded, 16 * (1 + PACK))
            centre(CEN_N2, 2, low_step, low_ready)
            dve.wait_ge(pe_prep, 1)
            nc.vector.tensor_copy(we2T[:, :], banks(2, P)).then_inc(prep, 1)
            dve.wait_ge(pe_prep, 2)
            nc.vector.tensor_tensor(shift_cols[:, :], banks(3, 1).to_broadcast([P, P]), cols[:, 1:2].to_broadcast([P, P]),
                                    ALU.add).then_inc(prep, 1)
            dve.wait_ge(ends_loaded, 16 * 3)
            for k, op in enumerate((ALU.min, ALU.max)):
                last = nc.vector.tensor_reduce(lohi[:, k, :], ends[:, :, :], AX.X, op)
            last.then_inc(prep, 1)
            dve.wait_ge(prep, 3)
            for k in range(2):
                for c in range(2):
                    last = nc.vector.tensor_scalar(spread_diag[:, k, c, :], ident[0:HALF, 0:HALF], lohi[:, k, c:c + 1], None, ALU.mult)
            last.then_inc(prep, 1)
            dve.wait_ge(low_ready, 1)
            dve.wait_ge(wedge_clear, 1)
            for q in range(PACK):
                nc.vector.tensor_copy(wedge[q * DE:(q + 1) * DE, q, :], cen[q * DE:(q + 1) * DE, CEN_EDGE, :]).then_inc(prep, 1)
            dve.wait_ge(late_loaded, 16 * 9)
            dve.wait_ge(own_kept, GROUPS)
            nc.vector.tensor_copy(scale, vec[:, V_GE, :]).then_inc(prep, 1)
            nc.vector.tensor_scalar(neg, vec[:, V_BE, :], -1.0, None, ALU.mult).then_inc(prep, 1)
            dve.wait_ge(ramp_made, 1)
            nc.vector.tensor_copy(ramp, ramp_i[:, :]).then_inc(prep, 1)
            dve.wait_ge(pe_prep, 3)
            nc.vector.tensor_copy(fused[:, :], banks(4, H)).then_inc(prep, 1)
            dve.wait_ge(pe_prep, 4)
            nc.vector.tensor_copy(shift[:, :], banks(0, H)).then_inc(prep, 1)
            dve.wait_ge(pe_prep, 5)
            bounds = banks(6, 4 * HALF).rearrange("p (k c q) -> p k q c", k=2, c=2)
            nc.vector.tensor_copy(base[:, :].rearrange("p (q c) -> p q c", c=2), bounds[:, 0, :, :]).then_inc(prep, 1)
            done = 4 + PACK + 6
            dve.wait_ge(prep, done)
            nc.vector.tensor_copy(base_i[:, :], base[0:1, :])
            nc.vector.tensor_tensor(reach[:, :].rearrange("p (q c) -> p q c", c=2), bounds[0:1, 1, :, :],
                                    base[0:1, :].rearrange("p (q c) -> p q c", c=2), ALU.subtract).then_inc(prep, 1)
            dve.wait_ge(prep, done + 1)
            nc.vector.tensor_copy(reach_i[:, :], reach[:, :]).then_inc(prep, 1)
            dve.wait_ge(prep, done + 2)
            nc.vector.tensor_scalar(reach_i[:, :], reach_i[:, :], 5, None, ALU.arith_shift_right).then_inc(prep, 1)
            dve.wait_ge(prep, done + 3)
            nc.vector.tensor_scalar(reach_i[:, :], reach_i[:, :], 171, None, ALU.mult).then_inc(prep, 1)
            dve.wait_ge(prep, done + 4)
            nc.vector.tensor_scalar(more_i[:, :], reach_i[:, :], 9, None, ALU.arith_shift_right).then_inc(prep_ready, 1)
            dve.wait_ge(prep_ready, 1)
            dve.wait_ge(sums_cleared, 1 + CLEARS)

            windows = dve.alloc_register("dve_windows")
            dve.reg_mov(windows, 0)

            def make_onehot(b, r, s, signal):
                nc.vector.tensor_tensor(onehot[b][0:r, 0:s, :], ramp[0:r, :].unsqueeze(1).to_broadcast([r, s, W]),
                                        offs[b][0:r, 0:s].unsqueeze(2).to_broadcast([r, s, W]), ALU.is_equal).then_inc(signal, 1)

            def add_sums(c, b):
                r, s = size_of(c)
                dve.wait_ge(sums_ready, c + 1)
                if at_least(c, 1):
                    dve.wait_ge(sums_added, c)
                start = dve.value_load(base_i[0:1, bass.ds(c, 1)], min_val=0, max_val=N - 1)
                more = dve.value_load(more_i[0:1, bass.ds(c, 1)], min_val=0, max_val=MOST)
                window = acc[:, :, bass.ds(start, W)]
                sums = ps_sum[b][:, :].rearrange("p (k w) -> p k w", k=2)
                nc.vector.tensor_tensor(window, window, sums, ALU.add).then_inc(sums_added, 1)
                with dve.If(more > 0):
                    with dve.Fori(1, more + 1) as k:
                        dve.reg_add(windows, windows, 1)
                        w = dve.snap(windows)
                        dve.wait_ge(sums_added, c + 1)
                        nc.vector.tensor_scalar(offs[b][0:r, 0:s], offs[b][0:r, 0:s], -float(W), None, ALU.add).then_inc(more_offs, 1)
                        dve.wait_ge(more_offs, w)
                        make_onehot(b, r, s, more_onehot)
                        dve.wait_ge(more_sums, w)
                        far = nc.s_assert_within(start + k * W, 0, N - 1)
                        window = acc[:, :, bass.ds(far, W)]
                        nc.vector.tensor_tensor(window, window, sums, ALU.add).then_inc(more_added, 1)
                        dve.wait_ge(more_added, w)

            def normalise(c, b, beside):
                r, s = size_of(c)
                v, sd, rs, a, q = (small[b][0:r, k, 0:s] for k in range(5))
                dve.wait_ge(std_ready, c + 1)
                nc.vector.reciprocal(rs, sd).then_inc(root, 1)
                beside[0]()
                dve.wait_ge(var_ready, c + 1)
                dve.wait_ge(root, 4 * c + 1)
                nc.vector.scalar_tensor_tensor(a, v, -0.5, rs, ALU.mult, ALU.mult).then_inc(root, 1)
                beside[1]()
                dve.wait_ge(root, 4 * c + 2)
                nc.vector.tensor_tensor(q, a, rs, ALU.mult).then_inc(root, 1)
                dve.wait_ge(root, 4 * c + 3)
                nc.vector.scalar_tensor_tensor(rs, q, 1.5, rs, ALU.add, ALU.mult).then_inc(root, 1)
                if at_least(c, 2):
                    dve.wait_ge(sums_ready, c - 1)
                dve.wait_ge(root, 4 * c + 4)
                halves = (range(0, s // 2), range(s // 2, s))
                for part in halves:
                    for j in part:
                        last = nc.vector.scalar_tensor_tensor(msg[b][0:r, j, :], z[b][0:r, j, :], rs[:, j:j + 1], scale[0:r, :],
                                                              ALU.mult, ALU.mult)
                    last.then_inc(scaled, 1)
                for k, part in enumerate(halves):
                    dve.wait_ge(scaled, 2 * c + k + 1)
                    values = msg[b][0:r, part.start:part.stop, :]
                    nc.vector.tensor_tensor(values, values, neg[0:r, :].unsqueeze(1).to_broadcast([r, len(part), H]), ALU.max
                                            ).then_inc(message_ready, 1)

            def pre_norm(c, b, n):
                r, s = size_of(c)
                dve.wait_ge(edge_projected, c + 1)
                dve.wait_ge(gathered[b], 16 * SLOTS * n + 16 * s)
                nc.vector.tensor_tensor(z[b][0:r, 0:s, :], rows[b][0:r, 0:s, :],
                                        ps_edge[b][0:r, 0:s * H].rearrange("p (s h) -> p s h", s=s), ALU.add).then_inc(z_ready, 1)

            def place_receivers(c, b, n):
                r, s = size_of(c)
                dve.wait_ge(dst_loaded[b], 16 * (n + 1))
                nc.vector.tensor_scalar(offs[b][0:r, 0:s], dsts[b][0:r, 0:s], base[0:r, bass.ds(c, 1)], None, ALU.subtract
                                        ).then_inc(offs_ready, 1)
                dve.wait_ge(offs_ready, c + 1)
                make_onehot(b, r, s, onehot_ready)

            def nothing():
                pass

            def edge_step(c, b, n):
                if isinstance(c, int) and c == 0:
                    pre_norm(c, b, n)
                else:
                    normalise(c - 1, 1 - b, (nothing, lambda: pre_norm(c, b, n)))
                if at_least(c, 2):
                    add_sums(c - 2, b)
                place_receivers(c, b, n)
            chunks(dve, edge_step)
            normalise(CHUNKS - 1, (CHUNKS - 1) % 2, (nothing, nothing))
            for c in (CHUNKS - 2, CHUNKS - 1):
                add_sums(c, c % 2)
            dve.wait_ge(sums_added, CHUNKS)
            dve.sem_inc(totals_ready, 1)

            dve.wait_ge(cnt_turned, 1)
            nc.vector.tensor_scalar(any_in[:, :], ps_cnt, 1.0, None, ALU.min).then_inc(any_ready, 1)
            nc.vector.tensor_scalar(recip[:, :], ps_cnt, 1.0, None, ALU.max).then_inc(cnt_one, 1)
            dve.wait_ge(cnt_one, 1)
            nc.vector.reciprocal(recip[:, :], recip[:, :]).then_inc(recip_ready, 1)
            dve.wait_ge(recip_ready, 1)
            dve.wait_ge(any_ready, 1)
            dve.wait_ge(own_ready, GROUPS)

            def add_residual(g, b, n):
                dve.wait_ge(res_ready, g + 1)
                dve.wait_ge(out_projected, g + 1)
                if at_least(g, 2):
                    dve.wait_ge(out_written[b], 16 * n)
                nc.vector.tensor_tensor(o_t[b][:, :, :], ps_out[0:NR, :].rearrange("p (t c) -> p t c", t=GT),
                                        res[:, bass.ds(g * GT, GT), :], ALU.add).then_inc(out_ready, 1)

            def combine(g, b, beside=()):
                if at_least(g, 1):
                    dve.wait_ge(own_full, g)
                dve.wait_ge(agg_projected, g + 1)
                if at_least(g, 2):
                    dve.wait_ge(u_transposed, g - 1)
                for t in range(GT):
                    nc.vector.scalar_tensor_tensor(u[b][:, t, :], ps_agg[b][0:NR, t * H:(t + 1) * H], recip[:, bass.ds(g * GT + t, 1)],
                                                   nodes[:, g * GT + t, H:2 * H], ALU.mult, ALU.add).then_inc(u_ready, 1)
                    if t < len(beside):
                        beside[t]()

            def last_step(g, b, n):
                v, sd, rs, a, q = (small[b][0:NR, k, 0:GT] for k in range(5))

                def half():
                    dve.wait_ge(u_root, 4 * g + 1)
                    dve.wait_ge(u_var, g + 1)
                    nc.vector.scalar_tensor_tensor(a, v, -0.5, rs, ALU.mult, ALU.mult).then_inc(u_root, 1)

                def product():
                    dve.wait_ge(u_root, 4 * g + 2)
                    nc.vector.tensor_tensor(q, a, rs, ALU.mult).then_inc(u_root, 1)

                def newton():
                    dve.wait_ge(u_root, 4 * g + 3)
                    nc.vector.scalar_tensor_tensor(rs, q, 1.5, rs, ALU.add, ALU.mult).then_inc(u_root, 1)

                dve.wait_ge(u_std, g + 1)
                nc.vector.reciprocal(rs, sd).then_inc(u_root, 1)
                if g == GROUPS - 1:
                    half()
                    product()
                    newton()
                else:
                    combine(g + 1, 1 - b, (half, product, newton))
                dve.wait_ge(u_root, 4 * g + 4)
                nc.vector.tensor_tensor(u[b][:, :, :], u[b][:, :, :], rs.unsqueeze(2).to_broadcast([NR, GT, H]), ALU.mult).then_inc(u_done, 1)
                if at_least(g, 1):
                    add_residual(g - 1, 1 - b, n if b == 1 else n - 1)

            for t in range(GT):
                own = nodes[:, t, H:2 * H]
                last = nc.vector.scalar_tensor_tensor(own, shift[0:NR, :], any_in[:, t:t + 1], own, ALU.mult, ALU.add)
            last.then_inc(first_own, 1)
            dve.wait_ge(first_own, 1)
            combine(0, 0)
            last_groups(last_step)
            add_residual(GROUPS - 1, 1, GROUPS // 2 - 1)


_INS = ["x", "src", "dst", "edge_attr_32", "L0_gnn_We1", "L0_gnn_be1", "L0_gnn_ge1", "L0_gnn_ble1", "L0_gnn_We2", "L0_gnn_be2",
        "L0_gnn_Wn1", "L0_gnn_bn1", "L0_gnn_gn1", "L0_gnn_bln1", "L0_gnn_Wn2", "L0_gnn_bn2"]


def kernel(**inputs):
    import numpy as _np
    import concourse.bacc as _bacc
    from concourse import mybir as _mybir
    from concourse.bass_utils import run_bass_kernel_spmd as _run

    nc = _bacc.Bacc("TRN2", target_bir_lowering=False, num_devices=1)
    arrays, args = {}, []
    for name in _INS:
        a = _np.ascontiguousarray(inputs[name])
        arrays[f"in_{name}_dram"] = a
        args.append(nc.dram_tensor(f"in_{name}_dram", a.shape, _mybir.dt.from_np(a.dtype), kind="ExternalInput").ap())
    x = inputs["x"]
    args.append(nc.dram_tensor("out_0_dram", x.shape, _mybir.dt.from_np(_np.dtype(x.dtype)), kind="ExternalOutput").ap())
    graph_layer(nc, *args)
    r = _run(nc, [arrays], core_ids=[0])
    return r.results[0]["out_0_dram"]
```
